# Optimizing a Trainium2 kernel written in Bass

```python
import numpy as np
import jax
import jax.numpy as jnp

def _softmax(x, axis=-1):
    return jax.nn.softmax(x, axis=axis)

def _gelu(x):
    return jax.nn.gelu(x, approximate=True)

def _silu(x):
    return jax.nn.silu(x)

def _sigmoid(x):
    return jax.nn.sigmoid(x)

def _layernorm(x, axis=-1, eps=1e-05):
    m = jnp.mean(x, axis=axis, keepdims=True)
    v = jnp.var(x, axis=axis, keepdims=True)
    return (x - m) / jnp.sqrt(v + eps)

def _scatter_add(tgt, idx, src, axis=0):
    return tgt.at[idx].add(src)

def _segment_sum(src, seg, n):
    return jax.ops.segment_sum(src, seg, n)
kernel_name = 'mk_adaln_ffn_d1_seqx_r8_fed4b7'

def setup_inputs(seed: int=0):
    np.random.seed(seed)
    _w = jnp.asarray

    def _rec_inputs():
        import jax
        import jax.numpy as jnp
        _rk = jax.random.key(seed)
        x = 7.22e-05 + 1 * jax.random.normal(jax.random.fold_in(_rk, 1), (32, 32, 512), jnp.float32)
        _lenS = 32 - jax.random.randint(jax.random.fold_in(_rk, 7), (32,), 0, max(1, 32 // 4) + 1, jnp.int32)
        _lenS2 = 32 - jax.random.randint(jax.random.fold_in(_rk, 8), (32,), 0, max(1, 32 // 4) + 1, jnp.int32)
        itok_B_2_6 = jax.random.randint(jax.random.fold_in(_rk, 11), (32,), 2, 7, jnp.int32)
        return (x, itok_B_2_6)
    x, itok_B_2_6 = _rec_inputs()

    def _L0_cond_setup():
        import jax, jax.numpy as jnp
        import numpy as np
        B, N, H, F = (4, 64, 512, 1376)
        L, R, RANK = (1, 16, 16)
        SCALE = 0.5
        key = jax.random.key(seed)
        ks = jax.random.split(key, 12)
        nrm = lambda k, shape, fan: jax.random.normal(k, shape, jnp.float32) * fan ** (-0.5)
        inp = {'x': jax.random.normal(ks[0], (B, N, H), jnp.float32), 'W_gate': nrm(ks[1], (F, H), H), 'W_up': nrm(ks[2], (F, H), H), 'W_down': nrm(ks[3], (H, F), F), 'A_gate': nrm(ks[4], (L, R, RANK, H), H), 'B_gate': nrm(ks[5], (L, R, F, RANK), RANK), 'A_up': nrm(ks[6], (L, R, RANK, H), H), 'B_up': nrm(ks[7], (L, R, F, RANK), RANK), 'A_down': nrm(ks[8], (L, R, RANK, F), F), 'B_down': nrm(ks[9], (L, R, H, RANK), RANK), 'lora_indices': jax.random.randint(ks[10], (B,), 0, R), 'layer_idx': 0}
        return inp
    _L0_cond_all = _L0_cond_setup()
    _L0_cond_in = {k: v for k, v in _L0_cond_all.items() if k in ('W_gate', 'W_up', 'W_down', 'A_gate', 'B_gate', 'A_up', 'B_up', 'A_down', 'B_down')}
    del _L0_cond_all

    def _L0_ffn_setup():
        import jax, jax.numpy as jnp
        import numpy as np
        K_TOP = 8
        key = jax.random.key(seed)
        k1, k2, k3 = jax.random.split(key, 3)
        B, S, H, E = (4, 512, 512, 64)
        hidden_states = jax.random.normal(k1, (B, S, H), dtype=jnp.float32)
        router_weight = jax.random.normal(k2, (E, H), dtype=jnp.float32)
        router_bias = jnp.zeros((E,), dtype=jnp.float32)
        expert_bias = jax.random.normal(k3, (E, H), dtype=jnp.float32) * 0.1
        return {'hidden_states': hidden_states, 'router_weight': router_weight, 'router_bias': router_bias, 'expert_bias': expert_bias}
    _L0_ffn_all = _L0_ffn_setup()
    _L0_ffn_in = {k: v for k, v in _L0_ffn_all.items() if k in ('router_weight', 'router_bias', 'expert_bias')}
    del _L0_ffn_all
    return {'x': x, 'itok_B_2_6': itok_B_2_6, 'L0_cond_W_gate': _L0_cond_in['W_gate'], 'L0_cond_W_up': _L0_cond_in['W_up'], 'L0_cond_W_down': _L0_cond_in['W_down'], 'L0_cond_A_gate': _L0_cond_in['A_gate'], 'L0_cond_B_gate': _L0_cond_in['B_gate'], 'L0_cond_A_up': _L0_cond_in['A_up'], 'L0_cond_B_up': _L0_cond_in['B_up'], 'L0_cond_A_down': _L0_cond_in['A_down'], 'L0_cond_B_down': _L0_cond_in['B_down'], 'L0_ffn_router_weight': _L0_ffn_in['router_weight'], 'L0_ffn_router_bias': _L0_ffn_in['router_bias'], 'L0_ffn_expert_bias': _L0_ffn_in['expert_bias']}

def reference(x, itok_B_2_6, L0_cond_W_gate, L0_cond_W_up, L0_cond_W_down, L0_cond_A_gate, L0_cond_B_gate, L0_cond_A_up, L0_cond_B_up, L0_cond_A_down, L0_cond_B_down, L0_ffn_router_weight, L0_ffn_router_bias, L0_ffn_expert_bias):
    import jax
    import jax.numpy as jnp

    def _L0_cond_ref(x, W_gate, W_up, W_down, A_gate, B_gate, A_up, B_up, A_down, B_down, lora_indices, layer_idx):
        import jax, jax.numpy as jnp
        import numpy as np
        B, N, H, F = (4, 64, 512, 1376)
        L, R, RANK = (1, 16, 16)
        SCALE = 0.5

        def lora_add(base, inp, A, B):
            Ab = A[layer_idx][lora_indices]
            Bb = B[layer_idx][lora_indices]
            t = jnp.einsum('bri,bni->bnr', Ab, inp)
            return base + jnp.einsum('bor,bnr->bno', Bb, t) * SCALE
        gate = lora_add(jnp.einsum('bnh,fh->bnf', x, W_gate), x, A_gate, B_gate)
        up = lora_add(jnp.einsum('bnh,fh->bnf', x, W_up), x, A_up, B_up)
        act = jax.nn.silu(gate) * up
        down = lora_add(jnp.einsum('bnf,hf->bnh', act, W_down), act, A_down, B_down)
        return down

    def _L0_ffn_ref(hidden_states, router_weight, router_bias, expert_bias):
        import jax, jax.numpy as jnp
        import numpy as np
        K_TOP = 8
        B, S, H = hidden_states.shape
        E = router_weight.shape[0]
        T = B * S
        flat = hidden_states.reshape(T, H)
        logits = jnp.einsum('th,eh->te', flat, router_weight) + router_bias
        scores = jax.nn.softmax(logits, axis=-1)
        topk_w, topk_idx = jax.lax.top_k(scores, K_TOP)
        w_sum = topk_w.sum(axis=-1, keepdims=True)
        w_dense = jnp.zeros((T, E), dtype=scores.dtype).at[jnp.arange(T)[:, None], topk_idx].add(topk_w)
        bias_mix = jnp.einsum('te,eh->th', w_dense, expert_bias)
        out = flat * w_sum + bias_mix
        return out.reshape(B, S, H)
    x = x + _L0_ffn_ref(_L0_cond_ref(x, L0_cond_W_gate, L0_cond_W_up, L0_cond_W_down, L0_cond_A_gate, L0_cond_B_gate, L0_cond_A_up, L0_cond_B_up, L0_cond_A_down, L0_cond_B_down, itok_B_2_6, 0), L0_ffn_router_weight, L0_ffn_router_bias, L0_ffn_expert_bias)
    return x

_drawn_inputs = setup_inputs


def setup_inputs(seed=0):
    import zlib

    import numpy as np

    out = dict(_drawn_inputs(seed))
    spreads = {'L0_ffn_router_bias': (0.0, 0.1)}
    factors = {}
    for name, (base, spread) in spreads.items():
        noise = np.random.default_rng([zlib.crc32(name.encode()), seed]).standard_normal(out[name].shape)
        drawn = base * np.exp(spread * noise) if base else spread * noise
        out[name] = jnp.asarray(drawn.astype(out[name].dtype))
    for name, factor in factors.items():
        out[name] = (out[name] * factor).astype(out[name].dtype)
    return out
```

```python
from contextlib import ExitStack

import concourse.bass as bass
from concourse import mybir

F32 = mybir.dt.float32
F32R = mybir.dt.float32r
I32 = mybir.dt.int32
ALU = mybir.AluOpType
ACT = mybir.ActivationFunctionType
AX_X = mybir.AxisListType.X

P = 128
SEQ = 32
RANK = 16
ADAPTERS = 16
H = 512
F = 1376
E = 64
BATCH = 32
TOKENS = BATCH * SEQ
HC = H // P
FC = -(-F // P)
ROWS = P // RANK
GT = ROWS * SEQ
BT = 512
BLOCKS = TOKENS // BT
assert BLOCKS == 2
GB = BT // GT
BB = BT // SEQ
GROUPS = BLOCKS * GB
TC = BT // P
MATS = 2
GU = MATS * P
A_GU = MATS * HC * RANK
A_ROW = A_GU + FC * RANK
ALL = BLOCKS * FC
LORA_SCALE = 0.5

HEAD = 3
TAIL = 2
RS = 7



class Step:

    def __init__(self, blk, first, pair=None):
        run = 0 if pair is None else 2 * pair
        self.blk = blk
        self.known = first if pair is None else None
        self.j = first + run
        self.n = blk * FC + first + run
        self.slot = (blk * FC + first) % 2
        self.fills = (blk * FC + first) // 2 + 1 + (0 if pair is None else pair)
        self.first, self.pair = first, pair

    def shift(self, by):
        if self.known is not None and self.known + by >= FC:
            return Step(self.blk + 1, self.known + by - FC)
        return Step(self.blk, self.first + by, self.pair)

    def reuses(self):
        return self.known is None or self.n >= 2


def steps(eng, blk, body, head=HEAD, tail=TAIL):
    for j in range(head):
        body(Step(blk, j))
    with eng.Fori(0, (FC - head - tail) // 2, 1) as pair:
        body(Step(blk, head, pair))
        body(Step(blk, head + 1, pair))
    for j in range(FC - tail, FC):
        body(Step(blk, j))


T_ORDER = [(0, 0), (0, 1)]
for _b in range(BLOCKS):
    T_ORDER += [(_b + 1, 0), (_b, 2), (_b + 1, 1)] if _b + 1 < BLOCKS else [(_b, 2)]


def t_count(blk, m):
    return T_ORDER.index((blk, m)) + 1


def build(nc, x_t, adapter, adapter_rows, lane, masks, w_in, a_tab, b_tab, b_down_tab, router_t, router_bias,
          expert_bias, out_t):
    ctx = ExitStack()
    with ctx:
        def sb(name, shape, dt=F32):
            return ctx.enter_context(nc.sbuf_tensor(name, shape, dt))

        def bank(name):
            return ctx.enter_context(nc.psum_tensor(name, [P, 512], F32))

        def sem(name):
            return ctx.enter_context(nc.semaphore(name))

        x_raw = sb("x_raw", [P, HC, BT])
        w_raw = [sb(f"w_raw{s}", [P, HC * GU + H]) for s in range(2)]
        b_raw = [sb(f"b_raw{s}", [P, GB, GU]) for s in range(2)]
        bd_raw = sb("bd_raw", [P, GB, H])
        a_raw = sb("a_raw", [P, BATCH, A_ROW])
        x_s = [[sb(f"x_{k}{b}", [P, HC, BT], F32R) for k in ("hi", "lo")] for b in range(BLOCKS)]
        w_s = [[sb(f"w_{k}{s}", [P, HC * GU + H], F32R) for k in ("hi", "lo")] for s in range(2)]
        b_s = [[sb(f"b_{k}{s}", [P, GB, GU], F32R) for k in ("hi", "lo")] for s in range(2)]
        ad_s = [[sb(f"ad_{k}{s}", [P, BB * RANK], F32R) for k in ("hi", "lo")] for s in range(2)]
        bd_s = [sb(f"bd_{k}", [P, GB, H], F32R) for k in ("hi", "lo")]
        agu_s = [sb(f"agu_{k}", [P, MATS * HC, BB * RANK], F32R) for k in ("hi", "lo")]
        t_s = [[sb(f"t{m}_{k}", [P, BT], F32R) for k in ("hi", "lo")] for m in range(3)]
        act_s = [[sb(f"act_{k}{s}", [P, BT], F32R) for k in ("hi", "lo")] for s in range(2)]
        t_f = sb("t_f", [P, BT])
        silu = sb("silu", [P, BT])
        act_f = sb("act_f", [P, BT])
        down = sb("down", [P, HC, BT])
        logits = sb("logits", [P, TC, E])
        probs = sb("probs", [P, TC, E])
        rest = sb("rest", [P, TC, E])
        weights = sb("weights", [P, TC, E])
        row_max = sb("row_max", [P, TC])
        row_sum = sb("row_sum", [P, TC])
        row_inv = sb("row_inv", [P, TC])
        top8 = sb("top8", [P, TC, 8])
        w_t = sb("w_t", [E, BT])
        wsum = sb("wsum", [P, BT])
        mask = sb("mask", [P, GT + P])
        block_diag = mask[:, 0:GT]
        ident = mask[:, GT:GT + P]
        ones = sb("ones", [E, P])
        wr = sb("wr", [P, HC, E])
        rbias = sb("rbias", [P, E])
        ebias = sb("ebias", [E, H])
        lane_sb = sb("lane_sb", [P, 1], I32)
        rows_sb = sb("rows_sb", [P, GROUPS], I32)
        adapter_sb = sb("adapter_sb", [1, BATCH], I32)
        idx_base = sb("idx_base", [P, GROUPS], I32)
        two_chunks = sb("two_chunks", [P, GB], I32)
        idx = [sb(f"idx{s}", [P, GB], I32) for s in range(2)]

        gate_ps = bank("gate_ps")
        up_ps = bank("up_ps")
        down_ps = [bank(f"down_ps{h}") for h in range(HC)]
        td_ps = bank("td_ps")
        aux_ps = bank("aux_ps")

        x_loaded = [sem(f"x_loaded{b}") for b in range(BLOCKS)]
        x_again = [sem(f"x_again{b}") for b in range(BLOCKS)]
        w_loaded = [sem(f"w_loaded{s}") for s in range(2)]
        b_loaded = [sem(f"b_loaded{s}") for s in range(2)]
        bd_loaded = sem("bd_loaded")
        a_loaded = [sem(f"a_loaded{b}") for b in range(BLOCKS)]
        adapter_loaded = sem("adapter_loaded")
        rows_loaded = sem("rows_loaded")
        mask_loaded = sem("mask_loaded")
        small_loaded = sem("small_loaded")
        idx_ready = sem("idx_ready")
        step_ready = sem("step_ready")
        idx_taken = sem("idx_taken")
        idx_step = sem("idx_step")
        ones_ready = sem("ones_ready")
        x_hi = sem("x_hi")
        x_lo = sem("x_lo")
        agu_hi = sem("agu_hi")
        agu_lo = sem("agu_lo")
        gu_hi = sem("gu_hi")
        gu_lo = sem("gu_lo")
        d_hi = sem("d_hi")
        d_lo = sem("d_lo")
        bd_hi = sem("bd_hi")
        bd_lo = sem("bd_lo")
        t_masked = sem("t_masked")
        t_hi = sem("t_hi")
        t_lo = sem("t_lo")
        t_done = sem("t_done")
        gate_done = sem("gate_done")
        up_done = sem("up_done")
        down_done = sem("down_done")
        silu_done = sem("silu_done")
        mul_done = sem("mul_done")
        act_hi = sem("act_hi")
        act_lo = sem("act_lo")
        block_done = sem("block_done")
        down_v = sem("down_v")
        down_a = sem("down_a")
        logits_done = sem("logits_done")
        router_step = sem("router_step")
        exp_done = sem("exp_done")
        weights_done = sem("weights_done")
        wt_done = sem("wt_done")
        wt_copied = sem("wt_copied")
        wsum_done = sem("wsum_done")
        wsum_copied = sem("wsum_copied")
        scaled_v = sem("scaled_v")
        scaled_p = sem("scaled_p")
        added_v = sem("added_v")
        added_p = sem("added_p")
        mix_done = sem("mix_done")
        mixed = sem("mixed")
        stored = sem("stored")

        def raw(tile):
            return tile.bitcast(F32)

        block = ctx.enter_context(nc.Block())

        @block.sync
        def _(sp):
            sp.dma_start(adapter_sb[:, :], adapter).then_inc(adapter_loaded, 16)
            sp.dma_start(rows_sb[:, :], adapter_rows).then_inc(rows_loaded, 16)
            sp.dma_start(lane_sb[:, :], lane).then_inc(rows_loaded, 16)
            sp.dma_start(x_raw[:, :, :], x_t[:, :, 0:BT]).then_inc(x_loaded[0], 16)

            def load_w(st):
                if st.reuses():
                    sp.wait_ge(d_lo, st.n - 1)
                sp.dma_start(w_raw[st.slot][:, :], w_in[bass.ds(st.j, 1), :, :].rearrange("a p n -> (a p) n")).then_inc(w_loaded[st.slot], 16)

            def load_a(blk, b):
                which = sp.value_load(adapter_sb[0:1, bass.ds(b, 1)], min_val=0, max_val=ADAPTERS - 1)
                sp.dma_start(a_raw[:, bass.ds(b, 1), :].rearrange("p b n -> p (b n)"),
                             a_tab[bass.ds(which, 1), :, :].rearrange("a p n -> (a p) n")).then_inc(a_loaded[blk], 16)

            load_w(Step(0, 0))
            load_w(Step(0, 1))
            sp.dma_start(mask[:, :], masks).then_inc(mask_loaded, 16)
            sp.wait_ge(adapter_loaded, 16)
            with sp.Fori(0, BB, 1) as b:
                load_a(0, b)
            for dst, src in ((wr[:, :, :], router_t), (rbias[:, :], router_bias), (ebias[:, :], expert_bias)):
                sp.dma_start(dst, src).then_inc(small_loaded, 16)
            sp.wait_ge(x_lo, 1)
            sp.dma_start(x_raw[:, :, :], x_t[:, :, BT:2 * BT]).then_inc(x_loaded[1], 16)
            load_w(Step(0, 2))
            with sp.Fori(BB, BATCH, 1) as b:
                load_a(1, b)
            with sp.Fori(0, (FC - 3) // 2, 1) as pair:
                load_w(Step(0, 3, pair))
                load_w(Step(0, 4, pair))
            load_w(Step(1, 0))
            sp.wait_ge(x_lo, 2)
            sp.dma_start(x_raw[:, :, :], x_t[:, :, 0:BT]).then_inc(x_again[0], 16)
            with sp.Fori(0, (FC - 1) // 2, 1) as pair:
                load_w(Step(1, 1, pair))
                load_w(Step(1, 2, pair))
            for blk in range(BLOCKS):
                for h in range(HC):
                    sp.wait_ge(mixed, blk * HC + h + 1)
                    sp.dma_start(out_t[:, h:h + 1, blk * BT:(blk + 1) * BT], x_raw[:, h:h + 1, :]).then_inc(stored, 16)
                if blk == 0:
                    sp.wait_ge(stored, HC * 16)
                    sp.dma_start(x_raw[:, :, :], x_t[:, :, BT:2 * BT]).then_inc(x_again[1], 16)
            sp.wait_ge(stored, BLOCKS * HC * 16)

        def residual(tt, blk, h, sem_scaled, sem_added, wait, count):
            tt(down[:, h, :], down[:, h, :], wsum[:, :], ALU.mult).then_inc(sem_scaled, 1)
            wait(sem_scaled, count)
            tt(x_raw[:, h, :], x_raw[:, h, :], down[:, h, :], ALU.add).then_inc(sem_added, 1)

        @block.gpsimd
        def _(pool):
            nc.gpsimd.memset(two_chunks[:, :], 2 * ADAPTERS * RANK).then_inc(step_ready, 1)
            pool.wait_ge(step_ready, 1)
            pool.wait_ge(idx_ready, 2)

            def gather_b(st):
                if st.reuses():
                    pool.wait_ge(gu_lo, st.n - 1)
                at = idx[st.slot]
                if st.known is not None and st.known < 2:
                    nc.gpsimd.tensor_scalar(at[:, :], idx_base[:, st.blk * GB:(st.blk + 1) * GB], st.known * ADAPTERS * RANK,
                                            None, ALU.add).then_inc(idx_step, 1)
                else:
                    nc.gpsimd.tensor_tensor(at[:, :], at[:, :], two_chunks[:, :], ALU.add).then_inc(idx_step, 1)
                pool.wait_ge(idx_step, st.n + 1)
                pool.sem_inc(idx_taken, 1)
                for g in range(GB):
                    pool.indirect_dma_start(b_raw[st.slot][:, g, :], None, b_tab[:, :],
                                            bass.IndirectOffsetOnAxis(ap=at[:, g:g + 1], axis=0)).then_inc(b_loaded[st.slot], 16)

            def sum_residual(blk):
                pool.wait_ge(wsum_copied, blk + 1)
                pool.wait_ge(down_a, 2 * blk + 2)
                pool.wait_ge(x_again[blk], 16)
                for h in (2, 3):
                    residual(nc.gpsimd.tensor_tensor, blk, h, scaled_p, added_p, pool.wait_ge, 2 * blk + h - 1)

            for blk in range(BLOCKS):
                def body(st):
                    gather_b(st)
                    if st.known == 1:
                        if st.blk:
                            pool.wait_ge(bd_lo, st.blk)
                        for g in range(GB):
                            col = st.blk * GB + g
                            pool.indirect_dma_start(bd_raw[:, g, :], None, b_down_tab[:, :],
                                                    bass.IndirectOffsetOnAxis(ap=idx_base[:, col:col + 1], axis=0)).then_inc(bd_loaded, 16)
                    if st.blk and st.known == 4:
                        sum_residual(st.blk - 1)
                steps(pool, blk, body, head=5)
            sum_residual(BLOCKS - 1)

        def act_copy(dst, src):
            return nc.scalar.activation(dst, src, ACT.Copy)

        def a_down_of(blk, j):
            return a_raw[:, blk * BB:(blk + 1) * BB, bass.ds(A_GU + j * RANK, RANK)]

        def a_gu_of(blk, k):
            return a_raw[:, blk * BB:(blk + 1) * BB, k * RANK:(k + 1) * RANK]

        @block.scalar
        def _(act):
            def split_x(blk):
                act.wait_ge(x_loaded[blk], 16)
                act_copy(x_s[blk][0][:, :, :], x_raw[:, :, :]).then_inc(x_hi, 1)

            def split_agu(blk):
                act.wait_ge(a_loaded[blk], 16 * BB)
                if blk:
                    act.wait_ge(t_done, 2 * blk)
                for k in range(MATS * HC):
                    last = act_copy(agu_s[0][:, k, :].rearrange("p (b r) -> p b r", r=RANK), a_gu_of(blk, k))
                last.then_inc(agu_hi, 1)

            def split_gu(st):
                s, n = st.slot, st.n
                act.wait_ge(w_loaded[s], 16 * st.fills)
                if st.reuses():
                    act.wait_ge(up_done, n - 1)
                act_copy(w_s[s][0][:, 0:HC * GU], w_raw[s][:, 0:HC * GU])
                act.wait_ge(b_loaded[s], 16 * GB * st.fills)
                act_copy(b_s[s][0][:, :, :], b_raw[s][:, :, :]).then_inc(gu_hi, 1)

            def split_d(st):
                s, n = st.slot, st.n
                if st.reuses():
                    act.wait_ge(down_done, n - 1)
                act_copy(w_s[s][0][:, HC * GU:], w_raw[s][:, HC * GU:])
                act_copy(ad_s[s][0][:, :].rearrange("p (b r) -> p b r", r=RANK), a_down_of(st.blk, st.j)).then_inc(d_hi, 1)

            def t_head(blk, m):
                act.wait_ge(t_masked, t_count(blk, m))
                act_copy(t_s[m][0][:, :], t_f[:, :]).then_inc(t_hi, 1)

            def router_exp(blk):
                act.wait_ge(router_step, RS * blk + 3)
                nc.scalar.activation(probs[:, :, :], logits[:, :, :], ACT.Exp).then_inc(exp_done, 1)

            def copy_wt(blk):
                act.wait_ge(wt_done, blk + 1)
                act_copy(w_t[:, :], aux_ps[0:E, :]).then_inc(wt_copied, 1)

            def copy_wsum(blk):
                act.wait_ge(wsum_done, blk + 1)
                act_copy(wsum[:, :], aux_ps[:, :]).then_inc(wsum_copied, 1)

            split_x(0)
            split_gu(Step(0, 0))
            split_agu(0)
            t_head(0, 0)
            t_head(0, 1)
            for blk in range(BLOCKS):
                def body(st):
                    split_d(st)
                    if not (st.blk == BLOCKS - 1 and st.known == FC - 1):
                        split_gu(st.shift(1))
                    act.wait_ge(gate_done, st.n + 1)
                    nc.scalar.activation(silu[:, :], gate_ps[:, :], ACT.Silu).then_inc(silu_done, 1)
                    act.wait_ge(mul_done, st.n + 1)
                    act_copy(act_s[st.slot][0][:, :], act_f[:, :]).then_inc(act_hi, 1)
                    if st.blk == 0 and st.known == 1:
                        split_x(1)
                    if st.blk == 0 and st.known == 2:
                        split_agu(1)
                    if st.known == 2:
                        act.wait_ge(bd_loaded, 16 * GB * (st.blk + 1))
                        if st.blk:
                            act.wait_ge(block_done, st.blk)
                        act_copy(bd_s[0][:, :, :], bd_raw[:, :, :]).then_inc(bd_hi, 1)
                    if st.blk and st.known == 0:
                        router_exp(st.blk - 1)
                    if st.blk and st.known == 1:
                        copy_wt(st.blk - 1)
                        copy_wsum(st.blk - 1)
                steps(act, blk, body)
                if blk + 1 < BLOCKS:
                    t_head(blk + 1, 0)
                t_head(blk, 2)
                if blk + 1 < BLOCKS:
                    t_head(blk + 1, 1)
                act.wait_ge(block_done, blk + 1)
                for h in (2, 3):
                    act_copy(down[:, h, :], down_ps[h][:, :]).then_inc(down_a, 1)
            router_exp(BLOCKS - 1)
            copy_wt(BLOCKS - 1)
            copy_wsum(BLOCKS - 1)

        @block.vector
        def _(dve):
            def sub(dst, src, head):
                return nc.vector.tensor_tensor(dst, src, raw(head), ALU.subtract)

            def split_x(blk):
                dve.wait_ge(x_hi, blk + 1)
                sub(x_s[blk][1][:, :, :], x_raw[:, :, :], x_s[blk][0][:, :, :]).then_inc(x_lo, 1)

            def split_agu(blk):
                dve.wait_ge(agu_hi, blk + 1)
                for k in range(MATS * HC):
                    view = [t[:, k, :].rearrange("p (b r) -> p b r", r=RANK) for t in agu_s]
                    last = sub(view[1], a_gu_of(blk, k), view[0])
                last.then_inc(agu_lo, 1)

            def split_gu(st):
                s = st.slot
                dve.wait_ge(gu_hi, st.n + 1)
                sub(w_s[s][1][:, 0:HC * GU], w_raw[s][:, 0:HC * GU], w_s[s][0][:, 0:HC * GU])
                sub(b_s[s][1][:, :, :], b_raw[s][:, :, :], b_s[s][0][:, :, :]).then_inc(gu_lo, 1)

            def split_d(st):
                s = st.slot
                dve.wait_ge(d_hi, st.n + 1)
                sub(w_s[s][1][:, HC * GU:], w_raw[s][:, HC * GU:], w_s[s][0][:, HC * GU:])
                view = [t[:, :].rearrange("p (b r) -> p b r", r=RANK) for t in ad_s[s]]
                sub(view[1], a_down_of(st.blk, st.j), view[0]).then_inc(d_lo, 1)

            def t_split(src, blk, m):
                if t_count(blk, m) > 1:
                    dve.wait_ge(t_lo, t_count(blk, m) - 1)
                for g in range(GB):
                    cols = slice(g * GT, (g + 1) * GT)
                    last = nc.vector.tensor_tensor(t_f[:, cols], src[:, cols], block_diag, ALU.mult)
                last.then_inc(t_masked, 1)
                dve.wait_ge(t_hi, t_count(blk, m))
                sub(t_s[m][1][:, :], t_f[:, :], t_s[m][0][:, :]).then_inc(t_lo, 1)

            def tokens_experts(v):
                return v.unsqueeze(2).to_broadcast([P, TC, E])

            def router(blk):
                base = RS * blk
                dve.wait_ge(logits_done, blk + 1)
                dve.wait_ge(small_loaded, 48)
                nc.vector.tensor_tensor(logits[:, :, :], aux_ps[:, 0:TC * E].rearrange("p (c e) -> p c e", e=E),
                                        rbias[:, :].unsqueeze(1).to_broadcast([P, TC, E]), ALU.add).then_inc(router_step, 1)
                dve.wait_ge(router_step, base + 1)
                nc.vector.tensor_reduce(row_max[:, :], logits[:, :, :], AX_X, ALU.max).then_inc(router_step, 1)
                dve.wait_ge(router_step, base + 2)
                nc.vector.tensor_tensor(logits[:, :, :], logits[:, :, :], tokens_experts(row_max[:, :]),
                                        ALU.subtract).then_inc(router_step, 1)
                dve.wait_ge(exp_done, blk + 1)
                for c in range(TC):
                    nc.vector.max(top8[:, c, :], probs[:, c, :])
                nc.vector.tensor_reduce(row_sum[:, :], probs[:, :, :], AX_X, ALU.add).then_inc(router_step, 1)
                dve.wait_ge(router_step, base + 4)
                nc.vector.reciprocal(row_inv[:, :], row_sum[:, :]).then_inc(router_step, 1)
                for c in range(TC):
                    last = nc.vector.match_replace(rest[:, c, :], top8[:, c, :], probs[:, c, :], 0.0)
                last.then_inc(router_step, 1)
                dve.wait_ge(router_step, base + 6)
                nc.vector.tensor_tensor(rest[:, :, :], probs[:, :, :], rest[:, :, :], ALU.subtract).then_inc(router_step, 1)
                dve.wait_ge(router_step, base + RS)
                nc.vector.tensor_tensor(weights[:, :, :], rest[:, :, :], tokens_experts(row_inv[:, :]),
                                        ALU.mult).then_inc(weights_done, 1)

            def sum_residual(blk):
                dve.wait_ge(wsum_copied, blk + 1)
                dve.wait_ge(x_again[blk], 16)
                for h in (0, 1):
                    residual(nc.vector.tensor_tensor, blk, h, scaled_v, added_v, dve.wait_ge, 2 * blk + h + 1)

            def mix(blk, h):
                dve.wait_ge(mix_done, blk * HC + h + 1)
                if h < 2:
                    dve.wait_ge(added_v, 2 * blk + h + 1)
                else:
                    dve.wait_ge(added_p, 2 * blk + h - 1)
                nc.vector.tensor_tensor(x_raw[:, h, :], aux_ps[:, :], x_raw[:, h, :], ALU.add).then_inc(mixed, 1)

            dve.wait_ge(rows_loaded, 32)
            nc.vector.tensor_scalar(rows_sb[:, :], rows_sb[:, :], RANK, None, ALU.mult).then_inc(idx_ready, 1)
            nc.vector.memset(ones[:, :], 1.0).then_inc(ones_ready, 1)
            dve.wait_ge(idx_ready, 1)
            nc.vector.tensor_tensor(idx_base[:, :], rows_sb[:, :], lane_sb[:, :].to_broadcast([P, GROUPS]), ALU.add).then_inc(idx_ready, 1)
            split_x(0)
            split_gu(Step(0, 0))
            split_agu(0)
            dve.wait_ge(mask_loaded, 16)
            dve.wait_ge(t_done, 1)
            t_split(aux_ps, 0, 0)
            dve.wait_ge(t_done, 2)
            t_split(aux_ps, 0, 1)
            for blk in range(BLOCKS):
                def body(st):
                    if st.blk and st.known == 2:
                        sum_residual(st.blk - 1)
                    split_d(st)
                    if not (st.blk == BLOCKS - 1 and st.known == FC - 1):
                        split_gu(st.shift(1))
                    dve.wait_ge(silu_done, st.n + 1)
                    dve.wait_ge(up_done, st.n + 1)
                    if st.known is None or st.n >= 1:
                        dve.wait_ge(act_lo, st.n)
                    nc.vector.tensor_tensor(act_f[:, :], up_ps[:, :], silu[:, :], ALU.mult).then_inc(mul_done, 1)
                    dve.wait_ge(act_hi, st.n + 1)
                    sub(act_s[st.slot][1][:, :], act_f[:, :], act_s[st.slot][0][:, :]).then_inc(act_lo, 1)
                    if st.blk == 0 and st.known == 1:
                        split_x(1)
                    if st.blk == 0 and st.known == 2:
                        split_agu(1)
                    if st.known == 2:
                        dve.wait_ge(bd_hi, st.blk + 1)
                        sub(bd_s[1][:, :, :], bd_raw[:, :, :], bd_s[0][:, :, :]).then_inc(bd_lo, 1)
                    if st.blk and st.known == 0:
                        router(st.blk - 1)
                    if st.blk and st.known == 2:
                        for h in range(HC):
                            mix(st.blk - 1, h)
                steps(dve, blk, body)
                if blk + 1 < BLOCKS:
                    dve.wait_ge(t_done, 2 * blk + 3)
                    t_split(aux_ps, blk + 1, 0)
                dve.wait_ge(down_done, FC * (blk + 1))
                t_split(td_ps, blk, 2)
                if blk + 1 < BLOCKS:
                    dve.wait_ge(t_done, 2 * blk + 4)
                    t_split(aux_ps, blk + 1, 1)
                dve.wait_ge(block_done, blk + 1)
                for h in (0, 1):
                    nc.vector.tensor_copy(down[:, h, :], down_ps[h][:, :]).then_inc(down_v, 1)
            router(BLOCKS - 1)
            sum_residual(BLOCKS - 1)
            for h in range(HC):
                mix(BLOCKS - 1, h)

        @block.tensor
        def _(pe):
            def three(out, w, x, start=False, stop=False):
                pe.matmul(out, w[0], x[0], start=start, stop=False, skip_group_check=True)
                pe.matmul(out, w[0], x[1], start=False, stop=False, skip_group_check=True)
                return pe.matmul(out, w[1], x[0], start=False, stop=stop, skip_group_check=True)

            def both(pair, *at):
                return [t[at] for t in pair]

            ALLP = slice(None)

            def a_x(blk, m):
                if m == 0:
                    pe.wait_ge(agu_lo, blk + 1)
                    pe.wait_ge(x_lo, blk + 1)
                    if blk:
                        pe.wait_ge(t_masked, t_count(blk - 1, 1))
                else:
                    pe.wait_ge(t_masked, t_count(blk, 0))
                for g in range(GB):
                    for c in range(HC):
                        last = three(aux_ps[:, g * GT:(g + 1) * GT],
                                     both(agu_s, ALLP, m * HC + c, slice(g * P, (g + 1) * P)),
                                     both(x_s[blk], ALLP, c, slice(g * GT, (g + 1) * GT)),
                                     start=(c == 0), stop=(c == HC - 1))
                last.then_inc(t_done, 1)

            def project(blk, m, s, out):
                for c in range(HC):
                    at = c * GU + m * P
                    three(out[:, :], both(w_s[s], ALLP, slice(at, at + P)), both(x_s[blk], ALLP, c, ALLP), start=(c == 0))
                for g in range(GB):
                    cols = slice(g * GT, (g + 1) * GT)
                    last = three(out[:, cols], both(b_s[s], ALLP, g, slice(m * P, (m + 1) * P)), both(t_s[m], ALLP, cols),
                                 stop=(g == GB - 1))
                return last

            def gate_up(st):
                pe.wait_ge(gu_lo, st.n + 1)
                if st.known == 0:
                    pe.wait_ge(t_lo, t_count(st.blk, 1))
                later = st.known is None or st.n >= 1
                if later:
                    pe.wait_ge(silu_done, st.n)
                project(st.blk, 0, st.slot, gate_ps).then_inc(gate_done, 1)
                if later:
                    pe.wait_ge(mul_done, st.n)
                project(st.blk, 1, st.slot, up_ps).then_inc(up_done, 1)

            def down_step(st):
                s = st.slot
                pe.wait_ge(d_lo, st.n + 1)
                pe.wait_ge(act_lo, st.n + 1)
                first = st.known == 0
                if first and st.blk:
                    pe.wait_ge(down_v, 2 * st.blk)
                    pe.wait_ge(down_a, 2 * st.blk)
                for h in range(HC):
                    at = HC * GU + h * P
                    three(down_ps[h][:, :], both(w_s[s], ALLP, slice(at, at + P)), both(act_s[s], ALLP, ALLP), start=first)
                for g in range(GB):
                    cols = slice(g * GT, (g + 1) * GT)
                    last = three(td_ps[:, cols], both(ad_s[s], ALLP, slice(g * P, (g + 1) * P)), both(act_s[s], ALLP, cols),
                                 start=first and g == 0)
                last.then_inc(down_done, 1)

            def b_down(blk):
                pe.wait_ge(bd_lo, blk + 1)
                pe.wait_ge(t_lo, t_count(blk, 2))
                for h in range(HC):
                    for g in range(GB):
                        cols = slice(g * GT, (g + 1) * GT)
                        last = three(down_ps[h][:, cols], both(bd_s, ALLP, g, slice(h * P, (h + 1) * P)), both(t_s[2], ALLP, cols),
                                     stop=True)
                last.then_inc(block_done, 1)

            def router_logits(blk):
                pe.wait_ge(down_v, 2 * blk + 2)
                pe.wait_ge(down_a, 2 * blk + 2)
                pe.wait_ge(small_loaded, 48)
                for t in range(TC):
                    for c in range(HC):
                        last = pe.matmul(aux_ps[:, t * E:(t + 1) * E], down[:, c, t * P:(t + 1) * P], wr[:, c, :],
                                         start=(c == 0), stop=(c == HC - 1))
                last.then_inc(logits_done, 1)

            def turn_weights(blk):
                pe.wait_ge(weights_done, blk + 1)
                for t in range(TC):
                    last = pe.transpose(aux_ps[0:E, t * P:(t + 1) * P], weights[:, t, :], ident)
                last.then_inc(wt_done, 1)

            def weight_sums(blk):
                pe.wait_ge(wt_copied, blk + 1)
                pe.wait_ge(ones_ready, 1)
                pe.matmul(aux_ps[:, :], ones[:, :], w_t[:, :], start=True, stop=True).then_inc(wsum_done, 1)

            def bias_mix(blk, h):
                if h == 0:
                    pe.wait_ge(wsum_copied, blk + 1)
                else:
                    pe.wait_ge(mixed, blk * HC + h)
                pe.matmul(aux_ps[:, :], ebias[:, h * P:(h + 1) * P], w_t[:, :], start=True, stop=True).then_inc(mix_done, 1)

            a_x(0, 0)
            a_x(0, 1)
            for blk in range(BLOCKS):
                def body(st):
                    gate_up(st)
                    if st.known != 0:
                        down_step(st.shift(-1))
                    elif st.blk:
                        router_logits(st.blk - 1)
                    if st.blk and st.known == 1:
                        turn_weights(st.blk - 1)
                        weight_sums(st.blk - 1)
                    if st.blk and st.known == 2:
                        for h in range(HC):
                            bias_mix(st.blk - 1, h)
                steps(pe, blk, body, tail=0)
                if blk + 1 < BLOCKS:
                    a_x(blk + 1, 0)
                down_step(Step(blk, FC - 1))
                if blk + 1 < BLOCKS:
                    a_x(blk + 1, 1)
                b_down(blk)
            router_logits(BLOCKS - 1)
            turn_weights(BLOCKS - 1)
            weight_sums(BLOCKS - 1)
            for h in range(HC):
                bias_mix(BLOCKS - 1, h)


def kernel(**inputs):
    import numpy as np
    import concourse.bacc as bacc
    from concourse import mybir as mb
    from concourse.bass_utils import run_bass_kernel_spmd

    pre = "L0_cond_"
    get = {k: np.ascontiguousarray(v) for k, v in inputs.items()}
    pad = FC * P

    def hidden_major(w, width):
        out = np.zeros(w.shape[:-1] + (width,), w.dtype)
        out[..., :w.shape[-1]] = w
        return out

    x_t = get["x"].reshape(TOKENS, H).T.reshape(HC, P, TOKENS).transpose(1, 0, 2)
    gu = np.stack([hidden_major(get[pre + k].T, pad).reshape(HC, P, FC, P) for k in ("W_gate", "W_up")])
    gu = gu.transpose(3, 2, 1, 0, 4).reshape(FC, P, HC * GU)
    wd = hidden_major(get[pre + "W_down"], pad).T.reshape(FC, P, H)
    w_in = np.concatenate([gu, wd], axis=2)
    a_gu = np.stack([get[pre + k][0].reshape(ADAPTERS, RANK, HC, P) for k in ("A_gate", "A_up")], axis=1)
    a_gu = a_gu.transpose(0, 4, 1, 3, 2).reshape(ADAPTERS, P, A_GU)
    a_down = hidden_major(get[pre + "A_down"][0], pad).reshape(ADAPTERS, RANK, FC, P)
    a_down = a_down.transpose(0, 3, 2, 1).reshape(ADAPTERS, P, FC * RANK)
    a_tab = np.concatenate([a_gu, a_down], axis=2)
    b_gu = np.stack([hidden_major(get[pre + k][0].transpose(0, 2, 1), pad).reshape(ADAPTERS * RANK, FC, P)
                     for k in ("B_gate", "B_up")], axis=2)
    b_tab = b_gu.transpose(1, 0, 2, 3).reshape(FC * ADAPTERS * RANK, GU)
    b_down = get[pre + "B_down"][0].transpose(0, 2, 1).reshape(ADAPTERS * RANK, H)
    adapter = get["itok_B_2_6"].reshape(1, BATCH)
    adapter_rows = np.repeat(adapter[0], RANK).reshape(GROUPS, P).T
    lane = (np.arange(P) % RANK).astype(np.int32).reshape(P, 1)
    row, col = np.arange(P)[:, None], np.arange(GT)[None, :]
    masks = np.concatenate([np.where(row // RANK == col // SEQ, LORA_SCALE, 0.0), np.eye(P)], axis=1).astype(np.float32)
    router_t = get["L0_ffn_router_weight"].T.reshape(HC, P, E).transpose(1, 0, 2)
    router_bias = np.broadcast_to(get["L0_ffn_router_bias"], (P, E))
    arrays = dict(x_t=x_t, adapter=adapter, adapter_rows=adapter_rows, lane=lane, masks=masks, w_in=w_in, a_tab=a_tab,
                  b_tab=b_tab, b_down_tab=b_down, router_t=router_t, router_bias=router_bias,
                  expert_bias=get["L0_ffn_expert_bias"])
    arrays = {k: np.ascontiguousarray(v) for k, v in arrays.items()}

    nc = bacc.Bacc("TRN2", target_bir_lowering=False, num_devices=1)
    args = {k: nc.dram_tensor(k, v.shape, mb.dt.from_np(v.dtype), kind="ExternalInput").ap() for k, v in arrays.items()}
    out = nc.dram_tensor("out_t", (P, HC, TOKENS), mb.dt.float32, kind="ExternalOutput").ap()
    build(nc, out_t=out, **args)
    got = run_bass_kernel_spmd(nc, [arrays], core_ids=[0]).results[0]["out_t"]
    return got.transpose(2, 1, 0).reshape(BATCH, SEQ, H)
```

```python
from contextlib import ExitStack

import concourse.bass as bass
from concourse import mybir

F32 = mybir.dt.float32
F32R = mybir.dt.float32r
I32 = mybir.dt.int32
ALU = mybir.AluOpType
ACT = mybir.ActivationFunctionType
AX_X = mybir.AxisListType.X

P = 128
SEQ = 32
RANK = 16
ADAPTERS = 16
H = 512
F = 1376
E = 64
BATCH = 32
TOKENS = BATCH * SEQ
HC = H // P
FC = -(-F // P)
ROWS = P // RANK
GT = ROWS * SEQ
BT = 512
BLOCKS = TOKENS // BT
assert BLOCKS == 2
GB = BT // GT
BB = BT // SEQ
GROUPS = BLOCKS * GB
TC = BT // P
MATS = 2
GU = MATS * P
A_GU = MATS * HC * RANK
A_ROW = A_GU + FC * RANK
ALL = BLOCKS * FC
LORA_SCALE = 0.5

HEAD = (3, 5)
TAIL = (0, 2)
RS = 6
A_POOL = 6
LOWEST = -3.4028235e38



class Step:

    def __init__(self, blk, first, pair=None):
        run = 0 if pair is None else 2 * pair
        self.blk = blk
        self.known = first if pair is None else None
        self.j = first + run
        self.n = blk * FC + first + run
        self.slot = (blk * FC + first) % 2
        self.fills = (blk * FC + first) // 2 + 1 + (0 if pair is None else pair)
        self.first, self.pair = first, pair

    def shift(self, by):
        if self.known is not None and self.known + by >= FC:
            return Step(self.blk + 1, self.known + by - FC)
        return Step(self.blk, self.first + by, self.pair)

    def reuses(self):
        return self.known is None or self.n >= 2


def steps(eng, blk, body, tail=None):
    head, tail = HEAD[blk], TAIL[blk] if tail is None else tail
    for j in range(head):
        body(Step(blk, j))
    with eng.Fori(0, (FC - head - tail) // 2, 1) as pair:
        body(Step(blk, head, pair))
        body(Step(blk, head + 1, pair))
    for j in range(FC - tail, FC):
        body(Step(blk, j))


T_ORDER = [(0, 0), (0, 1)]
for _b in range(BLOCKS):
    T_ORDER += [(_b + 1, 0), (_b, 2), (_b + 1, 1)] if _b + 1 < BLOCKS else [(_b, 2)]


def t_count(blk, m):
    return T_ORDER.index((blk, m)) + 1


def build(nc, x_t, adapter, adapter_rows, lane, masks, w_in, a_tab, b_tab, b_down_tab, router_t, router_bias,
          expert_bias, out_t):
    ctx = ExitStack()
    with ctx:
        def sb(name, shape, dt=F32):
            return ctx.enter_context(nc.sbuf_tensor(name, shape, dt))

        def bank(name):
            return ctx.enter_context(nc.psum_tensor(name, [P, 512], F32))

        def sem(name):
            return ctx.enter_context(nc.semaphore(name))

        x_raw = sb("x_raw", [P, HC, BT])
        w_raw = [sb(f"w_raw{s}", [P, HC * GU + H]) for s in range(2)]
        b_raw = [sb(f"b_raw{s}", [P, GB, GU]) for s in range(2)]
        bd_raw = sb("bd_raw", [P, GB, H])
        a_raw = sb("a_raw", [P, BATCH, A_ROW])
        x_s = [[sb(f"x_{k}{b}", [P, HC, BT], F32R) for k in ("hi", "lo")] for b in range(BLOCKS)]
        w_s = [[sb(f"w_{k}{s}", [P, HC * GU + H], F32R) for k in ("hi", "lo")] for s in range(2)]
        b_s = [[sb(f"b_{k}{s}", [P, GB, GU], F32R) for k in ("hi", "lo")] for s in range(2)]
        ad_s = [[sb(f"ad_{k}{s}", [P, BB * RANK], F32R) for k in ("hi", "lo")] for s in range(2)]
        bd_s = [sb(f"bd_{k}", [P, GB, H], F32R) for k in ("hi", "lo")]
        agu_s = [sb(f"agu_{k}", [P, MATS * HC, BB * RANK], F32R) for k in ("hi", "lo")]
        t_s = [[sb(f"t{m}_{k}", [P, BT], F32R) for k in ("hi", "lo")] for m in range(3)]
        act_s = [[sb(f"act_{k}{s}", [P, BT], F32R) for k in ("hi", "lo")] for s in range(2)]
        t_f = sb("t_f", [P, BT])
        silu = sb("silu", [P, BT])
        act_f = sb("act_f", [P, BT])
        down = sb("down", [P, HC, BT])
        logits = sb("logits", [P, TC, E])
        probs = sb("probs", [P, TC, E])
        rest = sb("rest", [P, TC, E])
        row_sum = sb("row_sum", [P, TC])
        row_inv = sb("row_inv", [P, TC])
        top8 = sb("top8", [P, TC, 8])
        w_t = sb("w_t", [2 * E, BT], F32R)
        wsum = sb("wsum", [P, BT])
        ebias = down[:, 0, :]
        mask = sb("mask", [P, GT + P])
        block_diag = mask[:, 0:GT]
        ident = mask[:, GT:GT + P]
        ident_r = sb("ident_r", [P, P], F32R)
        ones = sb("ones", [2 * E, P], F32R)
        wr = sb("wr", [P, HC, E])
        rbias = sb("rbias", [1, E])
        ebias_hi = sb("ebias_hi", [2 * E, H], F32R)
        ebias_lo = sb("ebias_lo", [E, H], F32R)
        lane_sb = sb("lane_sb", [P, 1], I32)
        rows_sb = sb("rows_sb", [P, GROUPS], I32)
        adapter_sb = sb("adapter_sb", [1, BATCH], I32)
        idx_base = sb("idx_base", [P, GROUPS], I32)
        two_chunks = sb("two_chunks", [P, GB], I32)
        idx = [sb(f"idx{s}", [P, GB], I32) for s in range(2)]

        gate_ps = bank("gate_ps")
        up_ps = bank("up_ps")
        down_ps = [bank(f"down_ps{h}") for h in range(HC)]
        td_ps = bank("td_ps")
        aux_ps = bank("aux_ps")

        x_first = sem("x_first")
        gu_early = [sem(f"gu_early{s}") for s in range(2)]
        early_hi = sem("early_hi")
        early_lo = sem("early_lo")
        a_loaded_p = sem("a_loaded_p")
        ident_ready = sem("ident_ready")
        ebias_hi_done = sem("ebias_hi_done")
        ebias_lo_done = sem("ebias_lo_done")
        x_loaded = [sem(f"x_loaded{b}") for b in range(BLOCKS)]
        x_again = sem("x_again")
        w_loaded = [sem(f"w_loaded{s}") for s in range(2)]
        b_loaded = [sem(f"b_loaded{s}") for s in range(2)]
        bd_loaded = sem("bd_loaded")
        a_loaded = [sem(f"a_loaded{b}") for b in range(BLOCKS)]
        adapter_loaded = sem("adapter_loaded")
        rows_loaded = sem("rows_loaded")
        mask_loaded = sem("mask_loaded")
        small_loaded = sem("small_loaded")
        idx_ready = sem("idx_ready")
        step_ready = sem("step_ready")
        idx_taken = sem("idx_taken")
        idx_step = sem("idx_step")
        ones_ready = sem("ones_ready")
        x_hi = sem("x_hi")
        x_lo = sem("x_lo")
        agu_hi = sem("agu_hi")
        agu_lo = sem("agu_lo")
        gu_hi = sem("gu_hi")
        gu_lo = sem("gu_lo")
        d_hi = sem("d_hi")
        d_lo = sem("d_lo")
        bd_hi = sem("bd_hi")
        bd_lo = sem("bd_lo")
        t_masked = sem("t_masked")
        t_hi = sem("t_hi")
        t_lo = sem("t_lo")
        t_done = sem("t_done")
        gate_done = sem("gate_done")
        up_done = sem("up_done")
        down_done = sem("down_done")
        td_done = sem("td_done")
        silu_done = sem("silu_done")
        mul_done = sem("mul_done")
        act_hi = sem("act_hi")
        act_lo = sem("act_lo")
        block_done = sem("block_done")
        down_v = sem("down_v")
        down_a = sem("down_a")
        logits_done = sem("logits_done")
        router_step = sem("router_step")
        exp_done = sem("exp_done")
        weights_done = sem("weights_done")
        wt_done = sem("wt_done")
        wt_hi = sem("wt_hi")
        wt_lo = sem("wt_lo")
        wsum_done = sem("wsum_done")
        wsum_copied = sem("wsum_copied")
        scaled_v = sem("scaled_v")
        scaled_p = sem("scaled_p")
        added_v = sem("added_v")
        added_p = sem("added_p")
        mix_done = sem("mix_done")
        mixed = sem("mixed")
        stored = sem("stored")

        def raw(tile):
            return tile.bitcast(F32)

        block = ctx.enter_context(nc.Block())

        @block.sync
        def _(sp):
            sp.dma_start(adapter_sb[:, :], adapter).then_inc(adapter_loaded, 16)
            sp.dma_start(x_raw[:, 0:1, :], x_t[:, 0:1, 0:BT]).then_inc(x_first, 16)

            def w_row(j):
                return w_in[bass.ds(j, 1), :, :].rearrange("a p n -> (a p) n")

            def load_w(st):
                if st.reuses():
                    sp.wait_ge(d_lo, st.n - 1)
                sp.dma_start(w_raw[st.slot][:, :], w_row(st.j)).then_inc(w_loaded[st.slot], 16)

            def load_a(start, count, loaded):
                which = [sp.value_load(adapter_sb[0:1, bass.ds(start + k, 1)], min_val=0, max_val=ADAPTERS - 1)
                         for k in range(count)]
                for k in range(count):
                    sp.dma_start(a_raw[:, bass.ds(start + k, 1), :].rearrange("p b n -> p (b n)"),
                                 a_tab[bass.ds(which[k], 1), :, :].rearrange("a p n -> (a p) n")).then_inc(loaded, 16)

            sp.dma_start(w_raw[0][:, 0:HC * GU], w_in[0, :, 0:HC * GU]).then_inc(gu_early[0], 16)
            sp.dma_start(rows_sb[:, :], adapter_rows).then_inc(rows_loaded, 16)
            sp.dma_start(lane_sb[:, :], lane).then_inc(rows_loaded, 16)
            sp.dma_start(x_raw[:, 1:, :], x_t[:, 1:, 0:BT]).then_inc(x_loaded[0], 16)
            sp.dma_start(w_raw[1][:, 0:HC * GU], w_in[1, :, 0:HC * GU]).then_inc(gu_early[1], 16)
            sp.wait_ge(adapter_loaded, 16)
            with sp.Fori(0, 2, 1) as part:
                load_a((BB - A_POOL) // 2 * part, (BB - A_POOL) // 2, a_loaded[0])
            sp.dma_start(mask[:, :], masks).then_inc(mask_loaded, 16)
            for s in range(2):
                sp.dma_start(w_raw[s][:, HC * GU:], w_in[s, :, HC * GU:]).then_inc(w_loaded[s], 16)
            load_w(Step(0, 2))
            for dst, src in ((wr[:, :, :], router_t), (rbias[:, :], router_bias), (ebias[0:E, :], expert_bias),
                             (ebias[E:2 * E, :], expert_bias)):
                sp.dma_start(dst, src).then_inc(small_loaded, 16)
            sp.wait_ge(early_lo, HC)
            sp.dma_start(x_raw[:, :, :], x_t[:, :, BT:2 * BT]).then_inc(x_loaded[1], 16)
            with sp.Fori(0, (FC - 3) // 2, 1) as pair:
                load_w(Step(0, 3, pair))
                load_w(Step(0, 4, pair))
                load_a(BB + 4 * pair, 4, a_loaded[1])
            load_w(Step(1, 0))
            sp.wait_ge(x_lo, 1)
            sp.dma_start(x_raw[:, :, :], x_t[:, :, 0:BT]).then_inc(x_again, 16)
            with sp.Fori(0, (FC - 1) // 2, 1) as pair:
                load_w(Step(1, 1, pair))
                load_w(Step(1, 2, pair))
            for blk in range(BLOCKS):
                result = down if blk == BLOCKS - 1 else x_raw
                for h in range(HC):
                    sp.wait_ge(mixed, blk * HC + h + 1)
                    sp.dma_start(out_t[:, h:h + 1, blk * BT:(blk + 1) * BT], result[:, h:h + 1, :]).then_inc(stored, 16)
            sp.wait_ge(stored, BLOCKS * HC * 16)

        @block.gpsimd
        def _(pool):
            nc.gpsimd.memset(two_chunks[:, :], 2 * ADAPTERS * RANK).then_inc(step_ready, 1)
            pool.wait_ge(step_ready, 1)
            pool.wait_ge(idx_ready, 2)

            def gather_b(st):
                if st.reuses():
                    pool.wait_ge(gu_lo, st.n - 1)
                at = idx[st.slot]
                if st.known is not None and st.known < 2:
                    nc.gpsimd.tensor_scalar(at[:, :], idx_base[:, st.blk * GB:(st.blk + 1) * GB], st.known * ADAPTERS * RANK,
                                            None, ALU.add).then_inc(idx_step, 1)
                else:
                    nc.gpsimd.tensor_tensor(at[:, :], at[:, :], two_chunks[:, :], ALU.add).then_inc(idx_step, 1)
                pool.wait_ge(idx_step, st.n + 1)
                pool.sem_inc(idx_taken, 1)
                for g in range(GB):
                    pool.indirect_dma_start(b_raw[st.slot][:, g, :], None, b_tab[:, :],
                                            bass.IndirectOffsetOnAxis(ap=at[:, g:g + 1], axis=0)).then_inc(b_loaded[st.slot], 16)

            def load_a(start, count):
                which = [pool.value_load(adapter_sb[0:1, bass.ds(start + k, 1)], min_val=0, max_val=ADAPTERS - 1)
                         for k in range(count)]
                for k in range(count):
                    pool.dma_start(a_raw[:, bass.ds(start + k, 1), :].rearrange("p b n -> p (b n)"),
                                   a_tab[bass.ds(which[k], 1), :, :].rearrange("a p n -> (a p) n")).then_inc(a_loaded_p, 16)

            def scale_rows(blk, h):
                nc.gpsimd.tensor_tensor(down[:, h, :], down[:, h, :], wsum[:, :], ALU.mult).then_inc(scaled_p, 1)

            def body(st):
                if st.known == 1 and st.blk == 0:
                    pool.wait_ge(adapter_loaded, 16)
                    with pool.Fori(0, 2, 1) as part:
                        load_a(BB - A_POOL + A_POOL // 2 * part, A_POOL // 2)
                gather_b(st)
                if st.known == 1:
                    if st.blk:
                        pool.wait_ge(bd_lo, st.blk)
                    for g in range(GB):
                        col = st.blk * GB + g
                        pool.indirect_dma_start(bd_raw[:, g, :], None, b_down_tab[:, :],
                                                bass.IndirectOffsetOnAxis(ap=idx_base[:, col:col + 1], axis=0)).then_inc(bd_loaded, 16)
                if st.blk and st.known == 4:
                    pool.wait_ge(wsum_copied, st.blk)
                    pool.wait_ge(down_a, 2 * st.blk)
                    pool.wait_ge(down_v, 2 * st.blk)
                    pool.wait_ge(x_again, 16)
                    for h in range(HC):
                        scale_rows(st.blk - 1, h)
                        pool.wait_ge(scaled_p, h + 1)
                        nc.gpsimd.tensor_tensor(x_raw[:, h, :], x_raw[:, h, :], down[:, h, :], ALU.add).then_inc(added_p, 1)

            for blk in range(BLOCKS):
                steps(pool, blk, body, tail=0)
            pool.wait_ge(wsum_copied, BLOCKS)
            pool.wait_ge(down_a, 2 * BLOCKS)
            pool.wait_ge(down_v, 2 * BLOCKS)
            for h in (2, 3):
                scale_rows(BLOCKS - 1, h)

        def act_copy(dst, src):
            return nc.scalar.activation(dst, src, ACT.Copy)

        def a_down_of(blk, j):
            return a_raw[:, blk * BB:(blk + 1) * BB, bass.ds(A_GU + j * RANK, RANK)]

        def a_gu_of(blk, m):
            at = a_raw[:, blk * BB:(blk + 1) * BB, m * HC * RANK:(m + 1) * HC * RANK]
            return at.rearrange("p b (c r) -> p c b r", r=RANK)

        def agu_at(k, m):
            return agu_s[k][:, m * HC:(m + 1) * HC, :].rearrange("p c (b r) -> p c b r", r=RANK)

        def gate_bank(st):
            return down_ps[2] if st.known == 1 and st.blk == 0 else gate_ps

        def up_bank(st):
            return down_ps[3] if st.known == 1 and st.blk == 0 else up_ps

        @block.scalar
        def _(act):
            def split_agu(blk):
                act.wait_ge(a_loaded[blk], 16 * (BB if blk else BB - A_POOL))
                if blk:
                    act.wait_ge(t_done, 2 * blk)
                if not blk:
                    act.wait_ge(a_loaded_p, 16 * A_POOL)
                for m in range(MATS):
                    act_copy(agu_at(0, m), a_gu_of(blk, m)).then_inc(agu_hi, 1)

            def split_gu(st):
                s, n = st.slot, st.n
                if not st.reuses():
                    act.wait_ge(b_loaded[s], 16 * GB)
                    act_copy(b_s[s][0][:, :, :], b_raw[s][:, :, :]).then_inc(gu_hi, 1)
                    return
                act.wait_ge(w_loaded[s], 16 * st.fills)
                if st.reuses():
                    act.wait_ge(up_done, n - 1)
                act_copy(w_s[s][0][:, 0:HC * GU], w_raw[s][:, 0:HC * GU])
                act.wait_ge(b_loaded[s], 16 * GB * st.fills)
                act_copy(b_s[s][0][:, :, :], b_raw[s][:, :, :]).then_inc(gu_hi, 1)

            def split_d(st):
                s, n = st.slot, st.n
                act.wait_ge(w_loaded[s], 16 * st.fills)
                if st.reuses():
                    act.wait_ge(down_done, n - 1)
                act_copy(w_s[s][0][:, HC * GU:], w_raw[s][:, HC * GU:])
                act_copy(ad_s[s][0][:, :].rearrange("p (b r) -> p b r", r=RANK), a_down_of(st.blk, st.j)).then_inc(d_hi, 1)

            def t_head(blk, m):
                act.wait_ge(t_masked, t_count(blk, m))
                act_copy(t_s[m][0][:, :], t_f[:, :]).then_inc(t_hi, 1)

            def router_exp(blk):
                act.wait_ge(router_step, RS * blk + 3)
                nc.scalar.activation(probs[:, :, :], logits[:, :, :], ACT.Exp).then_inc(exp_done, 1)

            def head_wt(blk):
                act.wait_ge(wt_done, blk + 1)
                act_copy(w_t[0:E, :], aux_ps[0:E, :]).then_inc(wt_hi, 1)

            def copy_wsum(blk):
                act.wait_ge(wsum_done, blk + 1)
                act_copy(wsum[:, :], (aux_ps if blk < BLOCKS - 1 else td_ps)[:, :]).then_inc(wsum_copied, 1)

            act.wait_ge(x_first, 16)
            for c in range(HC):
                if c == 1:
                    act.wait_ge(x_loaded[0], 16)
                act_copy(x_s[0][0][:, c, :], x_raw[:, c, :])
                if c == 0:
                    act.wait_ge(gu_early[0], 16)
                act_copy(w_s[0][0][:, c * GU:(c + 1) * GU], w_raw[0][:, c * GU:(c + 1) * GU]).then_inc(early_hi, 1)
            act.wait_ge(gu_early[1], 16)
            act_copy(w_s[1][0][:, 0:HC * GU], w_raw[1][:, 0:HC * GU]).then_inc(early_hi, 1)
            split_gu(Step(0, 0))
            split_agu(0)
            t_head(0, 0)
            t_head(0, 1)
            split_gu(Step(0, 1))
            for blk in range(BLOCKS):
                def body(st):
                    if st.blk and st.known == 2:
                        copy_wsum(st.blk - 1)
                    split_d(st)
                    if not (st.known == FC - 1 or st.known == 0 and not st.blk):
                        split_gu(st.shift(1))
                    act.wait_ge(gate_done, st.n + 1)
                    nc.scalar.activation(silu[:, :], gate_bank(st)[:, :], ACT.Silu).then_inc(silu_done, 1)
                    act.wait_ge(mul_done, st.n + 1)
                    act_copy(act_s[st.slot][0][:, :], act_f[:, :]).then_inc(act_hi, 1)
                    if st.blk == 0 and st.known == 2:
                        act.wait_ge(x_loaded[1], 16)
                        act_copy(x_s[1][0][:, :, :], x_raw[:, :, :]).then_inc(x_hi, 1)
                        act.wait_ge(small_loaded, 64)
                        act.wait_ge(mask_loaded, 16)
                        act_copy(ebias_hi[:, :], ebias[:, :]).then_inc(ebias_hi_done, 1)
                        act_copy(ident_r[:, :], ident).then_inc(ident_ready, 1)
                    if st.known == 2:
                        act.wait_ge(bd_loaded, 16 * GB * (st.blk + 1))
                        if st.blk:
                            act.wait_ge(block_done, HC * st.blk)
                        act_copy(bd_s[0][:, :, :], bd_raw[:, :, :]).then_inc(bd_hi, 1)
                    if st.blk and st.known == 0:
                        router_exp(st.blk - 1)
                    if st.blk and st.known == 1:
                        head_wt(st.blk - 1)
                steps(act, blk, body)
                if blk + 1 < BLOCKS:
                    split_agu(blk + 1)
                    t_head(blk + 1, 0)
                t_head(blk, 2)
                if blk + 1 < BLOCKS:
                    t_head(blk + 1, 1)
                for h in (0, 2):
                    act.wait_ge(block_done, HC * blk + h + 1)
                    act_copy(down[:, h, :], down_ps[h][:, :]).then_inc(down_a, 1)
            router_exp(BLOCKS - 1)
            head_wt(BLOCKS - 1)
            copy_wsum(BLOCKS - 1)

        @block.vector
        def _(dve):
            def sub(dst, src, head):
                return nc.vector.tensor_tensor(dst, src, raw(head), ALU.subtract)

            def split_agu(blk):
                for m in range(MATS):
                    dve.wait_ge(agu_hi, MATS * blk + m + 1)
                    sub(agu_at(1, m), a_gu_of(blk, m), agu_at(0, m)).then_inc(agu_lo, 1)

            def split_gu(st):
                s = st.slot
                dve.wait_ge(gu_hi, st.n + 1)
                if st.reuses():
                    sub(w_s[s][1][:, 0:HC * GU], w_raw[s][:, 0:HC * GU], w_s[s][0][:, 0:HC * GU])
                sub(b_s[s][1][:, :, :], b_raw[s][:, :, :], b_s[s][0][:, :, :]).then_inc(gu_lo, 1)

            def split_d(st):
                s = st.slot
                dve.wait_ge(d_hi, st.n + 1)
                sub(w_s[s][1][:, HC * GU:], w_raw[s][:, HC * GU:], w_s[s][0][:, HC * GU:])
                view = [t[:, :].rearrange("p (b r) -> p b r", r=RANK) for t in ad_s[s]]
                sub(view[1], a_down_of(st.blk, st.j), view[0]).then_inc(d_lo, 1)

            def t_split(src, blk, m):
                if t_count(blk, m) > 1:
                    dve.wait_ge(t_lo, t_count(blk, m) - 1)
                for g in range(GB):
                    cols = slice(g * GT, (g + 1) * GT)
                    last = nc.vector.tensor_tensor(t_f[:, cols], src[:, cols], block_diag, ALU.mult)
                last.then_inc(t_masked, 1)
                dve.wait_ge(t_hi, t_count(blk, m))
                sub(t_s[m][1][:, :], t_f[:, :], t_s[m][0][:, :]).then_inc(t_lo, 1)

            def router(blk):
                base = RS * blk
                sums = aux_ps[:, 0:TC * E].rearrange("p (c e) -> p c e", e=E)
                dve.wait_ge(logits_done, blk + 1)
                for c in range(TC):
                    last = nc.vector.max(top8[:, c, :], sums[:, c, :])
                last.then_inc(router_step, 1)
                dve.wait_ge(router_step, base + 1)
                nc.vector.tensor_tensor(logits[:, :, :], sums, top8[:, :, 0:1].to_broadcast([P, TC, E]),
                                        ALU.subtract).then_inc(router_step, 1)
                for c in range(TC):
                    last = nc.vector.match_replace(rest[:, c, :], top8[:, c, :], sums[:, c, :], LOWEST)
                last.then_inc(router_step, 1)
                dve.wait_ge(router_step, base + 3)
                nc.vector.tensor_tensor(rest[:, :, :], sums, rest[:, :, :], ALU.not_equal).then_inc(router_step, 1)
                dve.wait_ge(exp_done, blk + 1)
                nc.vector.tensor_reduce(row_sum[:, :], probs[:, :, :], AX_X, ALU.add).then_inc(router_step, 1)
                dve.wait_ge(router_step, base + 5)
                nc.vector.reciprocal(row_inv[:, :], row_sum[:, :]).then_inc(router_step, 1)
                dve.wait_ge(router_step, base + RS)
                for c in range(TC):
                    nc.vector.scalar_tensor_tensor(probs[:, c, :], probs[:, c, :], row_inv[:, c:c + 1], rest[:, c, :],
                                                   ALU.mult, ALU.mult).then_inc(weights_done, 1)

            def rest_wt(blk):
                dve.wait_ge(wt_hi, blk + 1)
                nc.vector.tensor_tensor(w_t[E:2 * E, :], aux_ps[0:E, :], raw(w_t[0:E, :]), ALU.subtract).then_inc(wt_lo, 1)

            def mix(blk, h):
                dve.wait_ge(mix_done, blk * HC + h + 1)
                dve.wait_ge(added_p, h + 1)
                nc.vector.tensor_tensor(x_raw[:, h, :], aux_ps[:, :], x_raw[:, h, :], ALU.add).then_inc(mixed, 1)

            dve.wait_ge(rows_loaded, 32)
            nc.vector.tensor_scalar(rows_sb[:, :], rows_sb[:, :], RANK, None, ALU.mult).then_inc(idx_ready, 1)
            nc.vector.memset(raw(ones[:, :]), 1.0).then_inc(ones_ready, 1)
            dve.wait_ge(idx_ready, 1)
            nc.vector.tensor_tensor(idx_base[:, :], rows_sb[:, :], lane_sb[:, :].to_broadcast([P, GROUPS]), ALU.add).then_inc(idx_ready, 1)
            for c in range(HC):
                dve.wait_ge(early_hi, c + 1)
                sub(x_s[0][1][:, c, :], x_raw[:, c, :], x_s[0][0][:, c, :])
                at = slice(c * GU, (c + 1) * GU)
                sub(w_s[0][1][:, at], w_raw[0][:, at], w_s[0][0][:, at]).then_inc(early_lo, 1)
            dve.wait_ge(early_hi, HC + 1)
            sub(w_s[1][1][:, 0:HC * GU], w_raw[1][:, 0:HC * GU], w_s[1][0][:, 0:HC * GU]).then_inc(early_lo, 1)
            split_gu(Step(0, 0))
            split_agu(0)
            dve.wait_ge(mask_loaded, 16)
            dve.wait_ge(t_done, 1)
            t_split(aux_ps, 0, 0)
            dve.wait_ge(t_done, 2)
            t_split(aux_ps, 0, 1)
            split_gu(Step(0, 1))
            for blk in range(BLOCKS):
                def body(st):
                    if st.blk and st.known == 3:
                        mix(st.blk - 1, 2)
                    split_d(st)
                    if not (st.known == FC - 1 or st.known == 0 and not st.blk):
                        split_gu(st.shift(1))
                    if st.blk and st.known == 2:
                        mix(st.blk - 1, 0)
                    if st.blk and st.known == 3:
                        mix(st.blk - 1, 3)
                    dve.wait_ge(silu_done, st.n + 1)
                    dve.wait_ge(up_done, st.n + 1)
                    if st.known is None or st.n >= 1:
                        dve.wait_ge(act_lo, st.n)
                    nc.vector.tensor_tensor(act_f[:, :], up_bank(st)[:, :], silu[:, :], ALU.mult).then_inc(mul_done, 1)
                    dve.wait_ge(act_hi, st.n + 1)
                    sub(act_s[st.slot][1][:, :], act_f[:, :], act_s[st.slot][0][:, :]).then_inc(act_lo, 1)
                    if st.blk == 0 and st.known == 2:
                        dve.wait_ge(x_hi, 1)
                        sub(x_s[1][1][:, :, :], x_raw[:, :, :], x_s[1][0][:, :, :]).then_inc(x_lo, 1)
                        dve.wait_ge(ebias_hi_done, 1)
                        sub(ebias_lo[:, :], ebias[0:E, :], ebias_hi[0:E, :]).then_inc(ebias_lo_done, 1)
                    if st.known == 2:
                        dve.wait_ge(bd_hi, st.blk + 1)
                        sub(bd_s[1][:, :, :], bd_raw[:, :, :], bd_s[0][:, :, :]).then_inc(bd_lo, 1)
                    if st.blk and st.known == 0:
                        router(st.blk - 1)
                    if st.blk and st.known == 1:
                        rest_wt(st.blk - 1)
                    if st.blk and st.known == 2:
                        mix(st.blk - 1, 1)
                steps(dve, blk, body)
                if blk + 1 < BLOCKS:
                    split_agu(blk + 1)
                if blk + 1 < BLOCKS:
                    dve.wait_ge(t_done, 2 * blk + 3)
                    t_split(aux_ps, blk + 1, 0)
                dve.wait_ge(td_done, GB * FC * (blk + 1))
                t_split(td_ps, blk, 2)
                if blk + 1 < BLOCKS:
                    dve.wait_ge(t_done, 2 * blk + 4)
                    t_split(aux_ps, blk + 1, 1)
                for h in (1, 3):
                    dve.wait_ge(block_done, HC * blk + h + 1)
                    nc.vector.tensor_copy(down[:, h, :], down_ps[h][:, :]).then_inc(down_v, 1)
            blk = BLOCKS - 1
            router(blk)
            rest_wt(blk)
            dve.wait_ge(wsum_copied, BLOCKS)
            dve.wait_ge(down_a, 2 * BLOCKS)
            for h in range(HC):
                if h < 2:
                    nc.vector.tensor_tensor(down[:, h, :], down[:, h, :], wsum[:, :], ALU.mult).then_inc(scaled_v, 1)
                    dve.wait_ge(scaled_v, h + 1)
                else:
                    dve.wait_ge(scaled_p, HC * blk + h - 1)
                dve.wait_ge(mix_done, HC * blk + h + 1)
                nc.vector.tensor_tensor(down[:, h, :], down_ps[h][:, :], down[:, h, :], ALU.add).then_inc(mixed, 1)

        @block.tensor
        def _(pe):
            def three(out, w, x, start=False, stop=False):
                pe.matmul(out, w[0], x[0], start=start, stop=False, skip_group_check=True)
                pe.matmul(out, w[0], x[1], start=False, stop=False, skip_group_check=True)
                return pe.matmul(out, w[1], x[0], start=False, stop=stop, skip_group_check=True)

            def both(pair, *at):
                return [t[at] for t in pair]

            ALLP = slice(None)

            def a_x(blk, m):
                if m == 0:
                    pe.wait_ge(agu_lo, MATS * blk + 1)
                    if blk:
                        pe.wait_ge(x_lo, blk)
                        pe.wait_ge(t_masked, t_count(blk - 1, 1))
                else:
                    pe.wait_ge(agu_lo, MATS * blk + 2)
                    pe.wait_ge(t_masked, t_count(blk, 0))
                for g in range(GB):
                    for c in range(HC):
                        last = three(aux_ps[:, g * GT:(g + 1) * GT],
                                     both(agu_s, ALLP, m * HC + c, slice(g * P, (g + 1) * P)),
                                     both(x_s[blk], ALLP, c, slice(g * GT, (g + 1) * GT)),
                                     start=(c == 0), stop=(c == HC - 1))
                last.then_inc(t_done, 1)

            def w_x(blk, m, s, out, c):
                at = c * GU + m * P
                three(out[:, :], both(w_s[s], ALLP, slice(at, at + P)), both(x_s[blk], ALLP, c, ALLP), start=(c == 0))

            def b_a_x(m, s, out):
                for g in range(GB):
                    cols = slice(g * GT, (g + 1) * GT)
                    last = three(out[:, cols], both(b_s[s], ALLP, g, slice(m * P, (m + 1) * P)), both(t_s[m], ALLP, cols),
                                 stop=(g == GB - 1))
                return last

            def project(blk, m, s, out):
                for c in range(HC):
                    w_x(blk, m, s, out, c)
                return b_a_x(m, s, out)

            def gate(st):
                pe.wait_ge(gu_lo, st.n + 1)
                if st.known == 0:
                    pe.wait_ge(t_lo, t_count(st.blk, 1))
                pe.wait_ge(silu_done, st.n)
                project(st.blk, 0, st.slot, gate_ps).then_inc(gate_done, 1)

            def up(st):
                pe.wait_ge(mul_done, st.n)
                project(st.blk, 1, st.slot, up_ps).then_inc(up_done, 1)

            def first_steps():
                for j in range(2):
                    st = Step(0, j)
                    for c in range(HC):
                        if c == 0 or j == 0:
                            pe.wait_ge(early_lo, (c if j == 0 else HC) + 1)
                        w_x(0, 0, st.slot, gate_bank(st), c)
                        w_x(0, 1, st.slot, up_bank(st), c)
                a_x(0, 0)
                a_x(0, 1)
                for j in range(2):
                    st = Step(0, j)
                    pe.wait_ge(gu_lo, j + 1)
                    if j == 0:
                        pe.wait_ge(t_lo, t_count(0, 0))
                    b_a_x(0, st.slot, gate_bank(st)).then_inc(gate_done, 1)
                    if j == 0:
                        pe.wait_ge(t_lo, t_count(0, 1))
                    b_a_x(1, st.slot, up_bank(st)).then_inc(up_done, 1)
                pe.wait_ge(silu_done, 2)
                pe.wait_ge(mul_done, 2)

            def down_step(st):
                s = st.slot
                pe.wait_ge(d_lo, st.n + 1)
                pe.wait_ge(act_lo, st.n + 1)
                first = st.known == 0
                if first and st.blk:
                    pe.wait_ge(down_v, 2 * st.blk)
                    pe.wait_ge(down_a, 2 * st.blk)
                for g in range(GB):
                    cols = slice(g * GT, (g + 1) * GT)
                    three(td_ps[:, cols], both(ad_s[s], ALLP, slice(g * P, (g + 1) * P)), both(act_s[s], ALLP, cols),
                          start=first and g == 0).then_inc(td_done, 1)
                for h in range(HC):
                    at = HC * GU + h * P
                    last = three(down_ps[h][:, :], both(w_s[s], ALLP, slice(at, at + P)), both(act_s[s], ALLP, ALLP), start=first)
                last.then_inc(down_done, 1)

            def b_down(blk):
                pe.wait_ge(bd_lo, blk + 1)
                pe.wait_ge(t_lo, t_count(blk, 2))
                for h in range(HC):
                    for g in range(GB):
                        cols = slice(g * GT, (g + 1) * GT)
                        last = three(down_ps[h][:, cols], both(bd_s, ALLP, g, slice(h * P, (h + 1) * P)), both(t_s[2], ALLP, cols),
                                     stop=True)
                    last.then_inc(block_done, 1)

            def router_logits(blk):
                pe.wait_ge(small_loaded, 64)
                pe.wait_ge(ones_ready, 1)
                pe.matmul(aux_ps[:, 0:TC * E].rearrange("p (t e) -> p t e", e=E), raw(ones[0:1, :]), rbias[:, :].rearrange("a (o e) -> a o e", o=1).to_broadcast([1, TC, E]),
                          start=True, stop=False, skip_group_check=True)
                for c in range(HC):
                    pe.wait_ge((down_a, down_v)[c % 2], 2 * blk + c // 2 + 1)
                    for t in range(TC):
                        last = pe.matmul(aux_ps[:, t * E:(t + 1) * E], down[:, c, t * P:(t + 1) * P], wr[:, c, :],
                                         start=False, stop=(c == HC - 1), skip_group_check=True)
                last.then_inc(logits_done, 1)

            def turn_weights(blk):
                for t in range(TC):
                    pe.wait_ge(weights_done, TC * blk + t + 1)
                    last = pe.transpose(aux_ps[0:E, t * P:(t + 1) * P], probs[:, t, :], ident)
                last.then_inc(wt_done, 1)

            def weight_sums(blk, out):
                pe.wait_ge(wt_lo, blk + 1)
                pe.matmul(out[:, :], ones[:, :], w_t[:, :], start=True, stop=True).then_inc(wsum_done, 1)

            def bias_mix(h, out, start):
                cols = slice(h * P, (h + 1) * P)
                pe.matmul(out[:, :], ebias_hi[:, cols], w_t[:, :], start=start, stop=False, skip_group_check=True)
                pe.matmul(out[:, :], ebias_lo[:, cols], w_t[0:E, :], start=False, stop=True,
                          skip_group_check=True).then_inc(mix_done, 1)

            def mix_earlier(blk, h):
                if h == 0:
                    pe.wait_ge(wsum_copied, blk + 1)
                    pe.wait_ge(ebias_lo_done, 1)
                else:
                    pe.wait_ge(mixed, blk * HC + h)
                bias_mix(h, aux_ps, True)

            first_steps()
            for blk in range(BLOCKS):
                def body(st):
                    if st.blk == 0 and st.known == 0:
                        return
                    early = st.blk == 0 and st.known == 1
                    if not early:
                        gate(st)
                    if st.blk and st.known in (2, 3):
                        mix_earlier(st.blk - 1, 0 if st.known == 2 else 3)
                    if not early:
                        up(st)
                    if st.blk and st.known == 0:
                        router_logits(st.blk - 1)
                    if st.blk and st.known == 1:
                        turn_weights(st.blk - 1)
                    if st.blk and st.known == 2:
                        mix_earlier(st.blk - 1, 1)
                    if st.known != 0:
                        down_step(st.shift(-1))
                    if st.blk and st.known == 1:
                        weight_sums(st.blk - 1, aux_ps)
                    if st.blk and st.known == 2:
                        mix_earlier(st.blk - 1, 2)
                steps(pe, blk, body, tail=0)
                if blk + 1 < BLOCKS:
                    a_x(blk + 1, 0)
                down_step(Step(blk, FC - 1))
                if blk + 1 < BLOCKS:
                    a_x(blk + 1, 1)
                b_down(blk)
            blk = BLOCKS - 1
            router_logits(blk)
            pe.wait_ge(ident_ready, 1)
            for h in range(HC):
                pe.matmul(down_ps[h][:, :], ident_r[:, :], x_s[blk][0][:, h, :], start=True, stop=False, skip_group_check=True)
                pe.matmul(down_ps[h][:, :], ident_r[:, :], x_s[blk][1][:, h, :], start=False, stop=False, skip_group_check=True)
            turn_weights(blk)
            weight_sums(blk, td_ps)
            for h in range(HC):
                bias_mix(h, down_ps[h], False)


def kernel(**inputs):
    import numpy as np
    import concourse.bacc as bacc
    from concourse import mybir as mb
    from concourse.bass_utils import run_bass_kernel_spmd

    pre = "L0_cond_"
    get = {k: np.ascontiguousarray(v) for k, v in inputs.items()}
    pad = FC * P

    def hidden_major(w, width):
        out = np.zeros(w.shape[:-1] + (width,), w.dtype)
        out[..., :w.shape[-1]] = w
        return out

    x_t = get["x"].reshape(TOKENS, H).T.reshape(HC, P, TOKENS).transpose(1, 0, 2)
    gu = np.stack([hidden_major(get[pre + k].T, pad).reshape(HC, P, FC, P) for k in ("W_gate", "W_up")])
    gu = gu.transpose(3, 2, 1, 0, 4).reshape(FC, P, HC * GU)
    wd = hidden_major(get[pre + "W_down"], pad).T.reshape(FC, P, H)
    w_in = np.concatenate([gu, wd], axis=2)
    a_gu = np.stack([get[pre + k][0].reshape(ADAPTERS, RANK, HC, P) for k in ("A_gate", "A_up")], axis=1)
    a_gu = a_gu.transpose(0, 4, 1, 3, 2).reshape(ADAPTERS, P, A_GU)
    a_down = hidden_major(get[pre + "A_down"][0], pad).reshape(ADAPTERS, RANK, FC, P)
    a_down = a_down.transpose(0, 3, 2, 1).reshape(ADAPTERS, P, FC * RANK)
    a_tab = np.concatenate([a_gu, a_down], axis=2)
    b_gu = np.stack([hidden_major(get[pre + k][0].transpose(0, 2, 1), pad).reshape(ADAPTERS * RANK, FC, P)
                     for k in ("B_gate", "B_up")], axis=2)
    b_tab = b_gu.transpose(1, 0, 2, 3).reshape(FC * ADAPTERS * RANK, GU)
    b_down = get[pre + "B_down"][0].transpose(0, 2, 1).reshape(ADAPTERS * RANK, H)
    adapter = get["itok_B_2_6"].reshape(1, BATCH)
    adapter_rows = np.repeat(adapter[0], RANK).reshape(GROUPS, P).T
    lane = (np.arange(P) % RANK).astype(np.int32).reshape(P, 1)
    row, col = np.arange(P)[:, None], np.arange(GT)[None, :]
    masks = np.concatenate([np.where(row // RANK == col // SEQ, LORA_SCALE, 0.0), np.eye(P)], axis=1).astype(np.float32)
    router_t = get["L0_ffn_router_weight"].T.reshape(HC, P, E).transpose(1, 0, 2)
    router_bias = get["L0_ffn_router_bias"].reshape(1, E)
    arrays = dict(x_t=x_t, adapter=adapter, adapter_rows=adapter_rows, lane=lane, masks=masks, w_in=w_in, a_tab=a_tab,
                  b_tab=b_tab, b_down_tab=b_down, router_t=router_t, router_bias=router_bias,
                  expert_bias=get["L0_ffn_expert_bias"])
    arrays = {k: np.ascontiguousarray(v) for k, v in arrays.items()}

    nc = bacc.Bacc("TRN2", target_bir_lowering=False, num_devices=1)
    args = {k: nc.dram_tensor(k, v.shape, mb.dt.from_np(v.dtype), kind="ExternalInput").ap() for k, v in arrays.items()}
    out = nc.dram_tensor("out_t", (P, HC, TOKENS), mb.dt.float32, kind="ExternalOutput").ap()
    build(nc, out_t=out, **args)
    got = run_bass_kernel_spmd(nc, [arrays], core_ids=[0]).results[0]["out_t"]
    return got.transpose(2, 1, 0).reshape(BATCH, SEQ, H)
```

```python
from contextlib import ExitStack

import concourse.bass as bass
from concourse import mybir

F32 = mybir.dt.float32
F32R = mybir.dt.float32r
I32 = mybir.dt.int32
ALU = mybir.AluOpType
ACT = mybir.ActivationFunctionType
AX_X = mybir.AxisListType.X

P = 128
SEQ = 32
RANK = 16
ADAPTERS = 16
H = 512
F = 1376
E = 64
BATCH = 32
TOKENS = BATCH * SEQ
HC = H // P
FC = -(-F // P)
ROWS = P // RANK
GT = ROWS * SEQ
BT = 512
BLOCKS = TOKENS // BT
assert BLOCKS == 2
GB = BT // GT
BB = BT // SEQ
GROUPS = BLOCKS * GB
TC = BT // P
MATS = 2
GU = MATS * P
A_GU = MATS * HC * RANK
A_ROW = A_GU + FC * RANK
LORA_SCALE = 0.5

HEAD = (3, 5)
TAIL = (0, 2)
WARM_UP = 11
EARLY = 3
RS = 6
A_SYNC = 7
A_ORDER = (1, 0)
LOWEST = -3.4028235e38


class Step:

    def __init__(self, blk, first, pair=None):
        run = 0 if pair is None else 2 * pair
        self.blk = blk
        self.known = first if pair is None else None
        self.j = first + run
        self.n = blk * FC + first + run
        self.slot = (blk * FC + first) % 2
        self.fills = (blk * FC + first) // 2 + 1 + (0 if pair is None else pair)
        self.first, self.pair = first, pair

    def shift(self, by):
        if self.known is not None and self.known + by >= FC:
            return Step(self.blk + 1, self.known + by - FC)
        return Step(self.blk, self.first + by, self.pair)

    def early(self):
        return self.known is not None and self.n < EARLY

    def reuses(self):
        return self.known is None or self.n >= 2


def steps(eng, blk, body, tail=None):
    head, tail = HEAD[blk], TAIL[blk] if tail is None else tail
    for j in range(head):
        body(Step(blk, j))
    with eng.Fori(0, (FC - head - tail) // 2, 1) as pair:
        body(Step(blk, head, pair))
        body(Step(blk, head + 1, pair))
    for j in range(FC - tail, FC):
        body(Step(blk, j))


T_ORDER = [(0, 0), (0, 1)]
for _b in range(BLOCKS):
    T_ORDER += [(_b, 2)] + [(_b + 1, m) for m in range(MATS) if _b + 1 < BLOCKS]


def t_count(blk, m):
    return T_ORDER.index((blk, m)) + 1


class Part:

    def __init__(self, at, blk, start, tokens):
        self.at = at
        self.blk = blk
        self.cols = slice(start, start + tokens)
        self.chunks = range(start // P, (start + tokens) // P)
        self.span = slice(start // P, (start + tokens) // P)
        self.turned = TC * blk + start // P
        self.last = blk == BLOCKS - 1

    def copied(self, h):
        if self.last:
            return 0, HC // 2 + HC * (self.at - 1) + h + 1
        return h % 2, h // 2 + 1


PARTS = [Part(0, 0, 0, BT)] + [Part(1 + g, 1, g * GT, GT) for g in range(GB)]


def build(nc, x_t, adapter, adapter_rows, lane, masks, w_in, a_tab, b_tab, b_down_tab, router_t, router_bias,
          expert_bias, out_t):
    ctx = ExitStack()
    with ctx:
        def sb(name, shape, dt=F32):
            return ctx.enter_context(nc.sbuf_tensor(name, shape, dt))

        def bank(name):
            return ctx.enter_context(nc.psum_tensor(name, [P, 512], F32))

        def sem(name):
            return ctx.enter_context(nc.semaphore(name))

        x_raw = sb("x_raw", [P, HC, BT])
        w_raw = [sb(f"w_raw{s}", [P, HC * GU + H]) for s in range(2)]
        b_raw = [sb(f"b_raw{s}", [P, GB, GU]) for s in range(2)]
        bd_raw = sb("bd_raw", [P, GB, H])
        a_raw = sb("a_raw", [P, BATCH, A_ROW])
        x_s = [[sb(f"x_{k}{b}", [P, HC, BT], F32R) for k in ("hi", "lo")] for b in range(BLOCKS)]
        w_s = [[sb(f"w_{k}{s}", [P, HC * GU + H], F32R) for k in ("hi", "lo")] for s in range(2)]
        b_s = [[sb(f"b_{k}{s}", [P, GB, GU], F32R) for k in ("hi", "lo")] for s in range(2)]
        ad_s = [[sb(f"ad_{k}{s}", [P, BB * RANK], F32R) for k in ("hi", "lo")] for s in range(2)]
        bd_s = [sb(f"bd_{k}", [P, GB, H], F32R) for k in ("hi", "lo")]
        agu_s = [sb(f"agu_{k}", [P, MATS * HC, BB * RANK], F32R) for k in ("hi", "lo")]
        t_s = [[sb(f"t{m}_{k}", [P, BT], F32R) for k in ("hi", "lo")] for m in range(3)]
        act_s = [[sb(f"act_{k}{s}", [P, BT], F32R) for k in ("hi", "lo")] for s in range(2)]
        t_f = sb("t_f", [P, BT])
        silu = sb("silu", [P, BT])
        act_f = sb("act_f", [P, BT])
        down = sb("down", [P, HC, BT])
        logits = sb("logits", [P, TC, E])
        probs = sb("probs", [P, TC, E])
        rest = sb("rest", [P, TC, E])
        row_sum = sb("row_sum", [P, TC])
        row_inv = sb("row_inv", [P, TC])
        top8 = sb("top8", [P, TC, 8])
        w_t = sb("w_t", [2 * E, BT], F32R)
        wsum = sb("wsum", [P, BT])
        ebias = down[:, 0, :]
        mask = sb("mask", [P, GT + P])
        block_diag = mask[:, 0:GT]
        ident = mask[:, GT:GT + P]
        ident_r = sb("ident_r", [P, P], F32R)
        ones = sb("ones", [2 * E, P], F32R)
        wr = sb("wr", [P, HC, E])
        rbias = sb("rbias", [1, E])
        ebias_hi = sb("ebias_hi", [2 * E, H], F32R)
        ebias_lo = sb("ebias_lo", [E, H], F32R)
        lane_sb = sb("lane_sb", [P, 1], I32)
        rows_sb = sb("rows_sb", [P, GROUPS], I32)
        adapter_sb = sb("adapter_sb", [1, BATCH], I32)
        idx_base = sb("idx_base", [P, GROUPS], I32)
        two_chunks = sb("two_chunks", [P, GB], I32)
        idx = [sb(f"idx{s}", [P, GB], I32) for s in range(2)]

        gate_ps = bank("gate_ps")
        up_ps = bank("up_ps")
        down_ps = [bank(f"down_ps{h}") for h in range(HC)]
        td_ps = bank("td_ps")
        aux_ps = bank("aux_ps")
        ax_ps = (aux_ps, td_ps)

        first_loaded = [sem(f"first_loaded{c}") for c in range(HC)]
        gu_early = [sem(f"gu_early{j}") for j in range(1, EARLY)]
        early_used = sem("early_used")
        early_hi = sem("early_hi")
        early_lo = sem("early_lo")
        ident_ready = sem("ident_ready")
        ebias_hi_done = sem("ebias_hi_done")
        ebias_lo_done = sem("ebias_lo_done")
        x_loaded = sem("x_loaded")
        x_again = sem("x_again")
        w_loaded = [sem(f"w_loaded{s}") for s in range(2)]
        b_loaded = [sem(f"b_loaded{s}") for s in range(2)]
        bd_loaded = sem("bd_loaded")
        a_early = [sem(f"a_early{g}") for g in range(GB)]
        a_early_rest = sem("a_early_rest")
        a_loaded = sem("a_loaded")
        adapter_loaded = sem("adapter_loaded")
        rows_loaded = sem("rows_loaded")
        mask_loaded = sem("mask_loaded")
        small_loaded = sem("small_loaded")
        idx_ready = sem("idx_ready")
        step_ready = sem("step_ready")
        idx_taken = sem("idx_taken")
        idx_step = sem("idx_step")
        ones_ready = sem("ones_ready")
        x_hi = sem("x_hi")
        x_lo = sem("x_lo")
        agu_hi = sem("agu_hi")
        agu_lo = sem("agu_lo")
        gu_hi = sem("gu_hi")
        gu_lo = sem("gu_lo")
        d_hi = sem("d_hi")
        d_lo = sem("d_lo")
        bd_hi = sem("bd_hi")
        bd_lo = sem("bd_lo")
        t_masked = sem("t_masked")
        t_hi = sem("t_hi")
        t_lo = sem("t_lo")
        t_done = sem("t_done")
        gate_done = sem("gate_done")
        up_done = sem("up_done")
        down_done = sem("down_done")
        td_done = sem("td_done")
        silu_done = sem("silu_done")
        mul_done = sem("mul_done")
        act_hi = sem("act_hi")
        act_lo = sem("act_lo")
        block_done = sem("block_done")
        down_v = sem("down_v")
        down_a = sem("down_a")
        logits_done = sem("logits_done")
        router_step = sem("router_step")
        exp_done = sem("exp_done")
        weights_done = sem("weights_done")
        wt_done = sem("wt_done")
        wt_hi = sem("wt_hi")
        wt_lo = sem("wt_lo")
        wsum_done = sem("wsum_done")
        wsum_copied = sem("wsum_copied")
        scaled_v = sem("scaled_v")
        scaled_p = sem("scaled_p")
        added_p = sem("added_p")
        mix_done = sem("mix_done")
        mixed = sem("mixed")
        stored = sem("stored")

        def raw(tile):
            return tile.bitcast(F32)

        block = ctx.enter_context(nc.Block())

        @block.sync
        def _(sp):
            sp.dma_start(adapter_sb[:, :], adapter).then_inc(adapter_loaded, 16)
            for c in range(HC):
                sp.dma_start(x_raw[:, c:c + 1, :], x_t[:, c:c + 1, 0:BT]).then_inc(first_loaded[c], 16)
                sp.dma_start(w_raw[0][:, c * GU:(c + 1) * GU], w_in[0, :, c * GU:(c + 1) * GU]).then_inc(first_loaded[c], 16)

            def w_row(j):
                return w_in[bass.ds(j, 1), :, :].rearrange("a p n -> (a p) n")

            def load_w(st):
                if st.reuses():
                    sp.wait_ge(d_lo, st.n - 1)
                sp.dma_start(w_raw[st.slot][:, :], w_row(st.j)).then_inc(w_loaded[st.slot], 16)

            def load_a(start, count, loaded):
                which = [sp.value_load(adapter_sb[0:1, bass.ds(start + k, 1)], min_val=0, max_val=ADAPTERS - 1)
                         for k in range(count)]
                for k in range(count):
                    sp.dma_start(a_raw[:, bass.ds(start + k, 1), :].rearrange("p b n -> p (b n)"),
                                 a_tab[bass.ds(which[k], 1), :, :].rearrange("a p n -> (a p) n")).then_inc(loaded, 16)

            sp.dma_start(rows_sb[:, :], adapter_rows).then_inc(rows_loaded, 16)
            sp.dma_start(lane_sb[:, :], lane).then_inc(rows_loaded, 16)
            sp.dma_start(w_raw[1][:, 0:HC * GU], w_in[1, :, 0:HC * GU]).then_inc(gu_early[0], 16)
            sp.wait_ge(adapter_loaded, 16)
            load_a(0, 4, a_early[0])
            sp.wait_ge(early_lo, HC)
            sp.dma_start(w_raw[0][:, 0:HC * GU], w_in[2, :, 0:HC * GU]).then_inc(gu_early[1], 16)
            load_a(4, A_SYNC - 4, a_early[0])
            sp.dma_start(mask[:, :], masks).then_inc(mask_loaded, 16)
            sp.dma_start(w_raw[0][:, HC * GU:], w_in[0, :, HC * GU:]).then_inc(w_loaded[0], 16)
            sp.dma_start(w_raw[1][:, HC * GU:], w_in[1, :, HC * GU:]).then_inc(w_loaded[1], 16)
            for dst, src in ((wr[:, :, :], router_t), (rbias[:, :], router_bias), (ebias[0:E, :], expert_bias),
                             (ebias[E:2 * E, :], expert_bias)):
                sp.dma_start(dst, src).then_inc(small_loaded, 16)
            sp.wait_ge(d_lo, 1)
            sp.dma_start(w_raw[0][:, HC * GU:], w_in[2, :, HC * GU:]).then_inc(w_loaded[0], 16)
            sp.dma_start(x_raw[:, :, :], x_t[:, :, BT:2 * BT]).then_inc(x_loaded, 16)
            with sp.Fori(0, (FC - 3) // 2, 1) as pair:
                load_w(Step(0, 3, pair))
                load_w(Step(0, 4, pair))
                load_a(BB + 4 * pair, 4, a_loaded)
            load_w(Step(1, 0))
            sp.wait_ge(x_lo, 1)
            sp.dma_start(x_raw[:, :, :], x_t[:, :, 0:BT]).then_inc(x_again, 16)
            with sp.Fori(0, (FC - 1) // 2, 1) as pair:
                load_w(Step(1, 1, pair))
                load_w(Step(1, 2, pair))
            for part in PARTS:
                result = down if part.last else x_raw
                out_cols = slice(part.blk * BT + part.cols.start, part.blk * BT + part.cols.stop)
                for h in range(0, HC, 2):
                    sp.wait_ge(mixed, part.at * HC + h + 2)
                    sp.dma_start(out_t[:, h:h + 2, out_cols], result[:, h:h + 2, part.cols]).then_inc(stored, 16)
            sp.wait_ge(stored, len(PARTS) * HC // 2 * 16)

        @block.gpsimd
        def _(pool):
            nc.gpsimd.memset(two_chunks[:, :], 2 * ADAPTERS * RANK).then_inc(step_ready, 1)
            pool.wait_ge(step_ready, 1)

            def gather_b(st):
                if st.reuses():
                    pool.wait_ge(gu_lo, st.n - 1)
                at = idx[st.slot]
                if st.known is not None and st.known < 2:
                    nc.gpsimd.tensor_scalar(at[:, :], idx_base[:, st.blk * GB:(st.blk + 1) * GB], st.known * ADAPTERS * RANK,
                                            None, ALU.add).then_inc(idx_step, 1)
                else:
                    nc.gpsimd.tensor_tensor(at[:, :], at[:, :], two_chunks[:, :], ALU.add).then_inc(idx_step, 1)
                pool.wait_ge(idx_step, st.n + 1)
                pool.sem_inc(idx_taken, 1)
                for g in range(GB):
                    pool.indirect_dma_start(b_raw[st.slot][:, g, :], None, b_tab[:, :],
                                            bass.IndirectOffsetOnAxis(ap=at[:, g:g + 1], axis=0)).then_inc(b_loaded[st.slot], 16)

            def load_a(start, count, loaded):
                which = [pool.value_load(adapter_sb[0:1, bass.ds(start + k, 1)], min_val=0, max_val=ADAPTERS - 1)
                         for k in range(count)]
                for k in range(count):
                    pool.dma_start(a_raw[:, bass.ds(start + k, 1), :].rearrange("p b n -> p (b n)"),
                                   a_tab[bass.ds(which[k], 1), :, :].rearrange("a p n -> (a p) n")).then_inc(loaded, 16)

            def scale_rows(part, h):
                rows = down[:, h, part.cols]
                nc.gpsimd.tensor_tensor(rows, rows, wsum[:, part.cols], ALU.mult).then_inc(scaled_p, 1)

            pool.wait_ge(adapter_loaded, 16)
            load_a(ROWS, 4, a_early[1])
            load_a(ROWS + 4, 4, a_early[1])
            load_a(A_SYNC, ROWS - A_SYNC, a_early_rest)
            pool.wait_ge(idx_ready, 2)

            def body(st):
                gather_b(st)
                if st.known == 1:
                    if st.blk:
                        pool.wait_ge(bd_lo, st.blk)
                    for g in range(GB):
                        col = st.blk * GB + g
                        pool.indirect_dma_start(bd_raw[:, g, :], None, b_down_tab[:, :],
                                                bass.IndirectOffsetOnAxis(ap=idx_base[:, col:col + 1], axis=0)).then_inc(bd_loaded, 16)
                if st.blk and st.known == 4:
                    pool.wait_ge(wsum_copied, 1)
                    pool.wait_ge(down_a, HC // 2)
                    pool.wait_ge(down_v, HC // 2)
                    pool.wait_ge(x_again, 16)
                    for h in range(HC):
                        scale_rows(PARTS[0], h)
                        pool.wait_ge(scaled_p, h + 1)
                        nc.gpsimd.tensor_tensor(x_raw[:, h, :], x_raw[:, h, :], down[:, h, :], ALU.add).then_inc(added_p, 1)

            for blk in range(BLOCKS):
                steps(pool, blk, body, tail=0)
            for part in PARTS[1:]:
                pool.wait_ge(wsum_copied, part.at + 1)
                pool.wait_ge(down_a, part.copied(HC - 1)[1])
                for h in range(2, HC):
                    scale_rows(part, h)

        def act_copy(dst, src):
            return nc.scalar.activation(dst, src, ACT.Copy)

        def a_down_of(blk, j):
            return a_raw[:, blk * BB:(blk + 1) * BB, bass.ds(A_GU + j * RANK, RANK)]

        def a_gu_of(blk, g):
            at = a_raw[:, blk * BB + g * ROWS:blk * BB + (g + 1) * ROWS, 0:A_GU]
            return at.rearrange("p b (c r) -> p c b r", r=RANK)

        def agu_at(k, g):
            return agu_s[k][:, :, g * P:(g + 1) * P].rearrange("p c (b r) -> p c b r", r=RANK)

        def by_chunk(bank):
            return bank[:, 0:TC * E].rearrange("p (t e) -> p t e", e=E)

        def sums_of(part):
            return by_chunk((aux_ps, gate_ps, td_ps)[part.at])

        def wsum_bank(part):
            return up_ps if part.last else aux_ps

        early_banks = ((gate_ps, up_ps), (down_ps[2], down_ps[3]), (down_ps[0], down_ps[1]))

        def gu_bank(st, m):
            return early_banks[st.known][m] if st.early() else (gate_ps, up_ps)[m]

        @block.scalar
        def _(act):
            def split_agu(blk):
                if blk:
                    act.wait_ge(a_loaded, 16 * BB)
                    act.wait_ge(t_done, 2 * blk)
                for g in A_ORDER:
                    if not blk:
                        act.wait_ge(a_early[g], 16 * (ROWS if g else A_SYNC))
                    if not blk and g == 0:
                        act.wait_ge(a_early_rest, 16 * (ROWS - A_SYNC))
                    act_copy(agu_at(0, g), a_gu_of(blk, g)).then_inc(agu_hi, 1)

            def split_gu(st):
                s, n = st.slot, st.n
                if st.reuses():
                    act.wait_ge(up_done, n - 1)
                if not st.early():
                    act.wait_ge(w_loaded[s], 16 * st.fills)
                    act_copy(w_s[s][0][:, 0:HC * GU], w_raw[s][:, 0:HC * GU])
                act.wait_ge(b_loaded[s], 16 * GB * st.fills)
                act_copy(b_s[s][0][:, :, :], b_raw[s][:, :, :]).then_inc(gu_hi, 1)

            def split_d(st):
                s, n = st.slot, st.n
                act.wait_ge(w_loaded[s], 16 * st.fills)
                if st.reuses():
                    act.wait_ge(down_done, n - 1)
                act_copy(w_s[s][0][:, HC * GU:], w_raw[s][:, HC * GU:])
                act_copy(ad_s[s][0][:, :].rearrange("p (b r) -> p b r", r=RANK), a_down_of(st.blk, st.j)).then_inc(d_hi, 1)

            def t_head(blk, m):
                act.wait_ge(t_masked, t_count(blk, m))
                act_copy(t_s[m][0][:, :], t_f[:, :]).then_inc(t_hi, 1)

            def router_exp(part):
                act.wait_ge(router_step, RS * part.at + 2)
                nc.scalar.activation(probs[:, part.span, :], logits[:, part.span, :], ACT.Exp).then_inc(exp_done, 1)

            def head_wt(part):
                act.wait_ge(wt_done, part.at + 1)
                act_copy(w_t[0:E, part.cols], aux_ps[0:E, part.cols]).then_inc(wt_hi, 1)

            def copy_wsum(part):
                act.wait_ge(wsum_done, 2 * part.at if part.last else 1)
                act_copy(wsum[:, part.cols], wsum_bank(part)[:, part.cols]).then_inc(wsum_copied, 1)

            def copy_down(part, rows):
                for h in rows:
                    act.wait_ge(block_done, HC * part.at + h + 1)
                    act_copy(down[:, h, part.cols], down_ps[h][:, part.cols]).then_inc(down_a, 1)

            def gated(st):
                act.wait_ge(gate_done, st.n + 1)
                nc.scalar.activation(silu[:, :], gu_bank(st, 0)[:, :], ACT.Silu).then_inc(silu_done, 1)

            def act_head(st):
                act.wait_ge(mul_done, st.n + 1)
                act_copy(act_s[st.slot][0][:, :], act_f[:, :]).then_inc(act_hi, 1)

            act.wait_ge(ones_ready, 1)
            nc.scalar.activation(silu[0:1, 0:1], raw(ones[0:1, 0:1]), ACT.Silu)
            for c in range(HC):
                act.wait_ge(first_loaded[c], 32)
                act_copy(x_s[0][0][:, c, :], x_raw[:, c, :])
                act_copy(w_s[0][0][:, c * GU:(c + 1) * GU], w_raw[0][:, c * GU:(c + 1) * GU]).then_inc(early_hi, 1)
            for j in range(1, EARLY):
                act.wait_ge(gu_early[j - 1], 16)
                if j == 2:
                    act.wait_ge(early_used, 1)
                act_copy(w_s[j % 2][0][:, 0:HC * GU], w_raw[j % 2][:, 0:HC * GU]).then_inc(early_hi, 1)
            split_agu(0)
            for j in range(2):
                split_gu(Step(0, j))
                split_d(Step(0, j))
            for m in range(MATS):
                t_head(0, m)
            gated(Step(0, 0))
            split_gu(Step(0, 2))
            act_head(Step(0, 0))
            gated(Step(0, 1))
            act_head(Step(0, 1))
            for blk in range(BLOCKS):
                def body(st):
                    if st.blk == 0 and st.known in (0, 1):
                        return
                    if st.blk and st.known == 2:
                        copy_wsum(PARTS[0])
                    if st.blk == 0 and st.known == 2:
                        gated(st)
                        split_gu(st.shift(1))
                        split_d(st)
                    else:
                        split_d(st)
                        if st.known != FC - 1:
                            split_gu(st.shift(1))
                        gated(st)
                    act_head(st)
                    if st.blk == 0 and st.known == 2:
                        act.wait_ge(x_loaded, 16)
                        act_copy(x_s[1][0][:, :, :], x_raw[:, :, :]).then_inc(x_hi, 1)
                        act.wait_ge(small_loaded, 64)
                        act.wait_ge(mask_loaded, 16)
                        act_copy(ebias_hi[:, :], ebias[:, :]).then_inc(ebias_hi_done, 1)
                        act_copy(ident_r[:, :], ident).then_inc(ident_ready, 1)
                    if st.known == 2:
                        act.wait_ge(bd_loaded, 16 * GB * (st.blk + 1))
                        if st.blk:
                            act.wait_ge(block_done, HC * st.blk)
                        act_copy(bd_s[0][:, :, :], bd_raw[:, :, :]).then_inc(bd_hi, 1)
                    if st.blk and st.known == 0:
                        router_exp(PARTS[0])
                    if st.blk and st.known == 1:
                        head_wt(PARTS[0])
                steps(act, blk, body)
                if blk + 1 < BLOCKS:
                    split_agu(blk + 1)
                    t_head(blk, 2)
                    for m in range(MATS):
                        t_head(blk + 1, m)
                    copy_down(PARTS[0], (0, 2))
            t_head(BLOCKS - 1, 2)
            copy_down(PARTS[1], range(HC))
            router_exp(PARTS[1])
            copy_down(PARTS[2], range(HC))
            head_wt(PARTS[1])
            router_exp(PARTS[2])
            copy_wsum(PARTS[1])
            head_wt(PARTS[2])
            copy_wsum(PARTS[2])

        @block.vector
        def _(dve):
            def sub(dst, src, head):
                return nc.vector.tensor_tensor(dst, src, raw(head), ALU.subtract)

            def split_agu(blk):
                for k, g in enumerate(A_ORDER):
                    dve.wait_ge(agu_hi, GB * blk + k + 1)
                    sub(agu_at(1, g), a_gu_of(blk, g), agu_at(0, g)).then_inc(agu_lo, 1)

            def split_gu(st):
                s = st.slot
                dve.wait_ge(gu_hi, st.n + 1)
                if not st.early():
                    sub(w_s[s][1][:, 0:HC * GU], w_raw[s][:, 0:HC * GU], w_s[s][0][:, 0:HC * GU])
                sub(b_s[s][1][:, :, :], b_raw[s][:, :, :], b_s[s][0][:, :, :]).then_inc(gu_lo, 1)

            def split_d(st):
                s = st.slot
                dve.wait_ge(d_hi, st.n + 1)
                sub(w_s[s][1][:, HC * GU:], w_raw[s][:, HC * GU:], w_s[s][0][:, HC * GU:])
                view = [t[:, :].rearrange("p (b r) -> p b r", r=RANK) for t in ad_s[s]]
                sub(view[1], a_down_of(st.blk, st.j), view[0]).then_inc(d_lo, 1)

            def t_split(src, blk, m):
                if t_count(blk, m) > 1:
                    dve.wait_ge(t_lo, t_count(blk, m) - 1)
                by_group = [t[:, :].rearrange("p (g n) -> p g n", n=GT) for t in (t_f, src)]
                diag = block_diag.rearrange("p (o n) -> p o n", o=1).to_broadcast([P, GB, GT])
                nc.vector.tensor_tensor(by_group[0], by_group[1], diag, ALU.mult).then_inc(t_masked, 1)
                dve.wait_ge(t_hi, t_count(blk, m))
                sub(t_s[m][1][:, :], t_f[:, :], t_s[m][0][:, :]).then_inc(t_lo, 1)

            def top_eight(part):
                base = RS * part.at
                sums = sums_of(part)
                dve.wait_ge(logits_done, part.at + 1)
                for c in part.chunks:
                    last = nc.vector.max(top8[:, c, :], sums[:, c, :])
                last.then_inc(router_step, 1)
                dve.wait_ge(router_step, base + 1)
                nc.vector.tensor_tensor(logits[:, part.span, :], sums[:, part.span, :],
                                        top8[:, part.span, 0:1].to_broadcast([P, len(part.chunks), E]),
                                        ALU.subtract).then_inc(router_step, 1)
                for c in part.chunks:
                    last = nc.vector.match_replace(rest[:, c, :], top8[:, c, :], sums[:, c, :], LOWEST)
                last.then_inc(router_step, 1)
                dve.wait_ge(router_step, base + 3)
                nc.vector.tensor_tensor(rest[:, part.span, :], sums[:, part.span, :], rest[:, part.span, :],
                                        ALU.not_equal).then_inc(router_step, 1)

            def softmax(part):
                base = RS * part.at
                dve.wait_ge(exp_done, part.at + 1)
                nc.vector.tensor_reduce(row_sum[:, part.span], probs[:, part.span, :], AX_X, ALU.add).then_inc(router_step, 1)
                dve.wait_ge(router_step, base + 5)
                nc.vector.reciprocal(row_inv[:, part.span], row_sum[:, part.span]).then_inc(router_step, 1)
                dve.wait_ge(router_step, base + RS)
                for c in part.chunks:
                    nc.vector.scalar_tensor_tensor(probs[:, c, :], probs[:, c, :], row_inv[:, c:c + 1], rest[:, c, :],
                                                   ALU.mult, ALU.mult).then_inc(weights_done, 1)

            def rest_wt(part):
                dve.wait_ge(wt_hi, part.at + 1)
                nc.vector.tensor_tensor(w_t[E:2 * E, part.cols], aux_ps[0:E, part.cols], raw(w_t[0:E, part.cols]),
                                        ALU.subtract).then_inc(wt_lo, 1)

            def mix(h):
                dve.wait_ge(mix_done, h + 1)
                dve.wait_ge(added_p, h + 1)
                nc.vector.tensor_tensor(x_raw[:, h, :], aux_ps[:, :], x_raw[:, h, :], ALU.add).then_inc(mixed, 1)

            def scale_last(part):
                dve.wait_ge(wsum_done, 2 * part.at + 1)
                dve.wait_ge(down_a, part.copied(1)[1])
                for h in range(2):
                    at = down[:, h, part.cols]
                    nc.vector.tensor_tensor(at, gate_ps[:, part.cols], at, ALU.mult).then_inc(scaled_v, 1)

            def mix_last(part):
                for h in range(HC):
                    dve.wait_ge(mix_done, HC * part.at + h + 1)
                    if h < 2:
                        dve.wait_ge(scaled_v, 2 * (part.at - 1) + h + 1)
                    else:
                        dve.wait_ge(scaled_p, HC + 2 * (part.at - 1) + h - 1)
                    at = down[:, h, part.cols]
                    nc.vector.tensor_tensor(at, down_ps[h][:, part.cols], at, ALU.add).then_inc(mixed, 1)

            def gated(st):
                dve.wait_ge(silu_done, st.n + 1)
                dve.wait_ge(up_done, st.n + 1)
                if st.known is None or st.n >= 1:
                    dve.wait_ge(act_lo, st.n)
                nc.vector.tensor_tensor(act_f[:, :], gu_bank(st, 1)[:, :], silu[:, :], ALU.mult).then_inc(mul_done, 1)

            def act_rest(st):
                dve.wait_ge(act_hi, st.n + 1)
                sub(act_s[st.slot][1][:, :], act_f[:, :], act_s[st.slot][0][:, :]).then_inc(act_lo, 1)

            nc.vector.memset(raw(ones[:, :]), 1.0).then_inc(ones_ready, 1)
            for c in range(HC):
                dve.wait_ge(early_hi, c + 1)
                sub(x_s[0][1][:, c, :], x_raw[:, c, :], x_s[0][0][:, c, :])
                at = slice(c * GU, (c + 1) * GU)
                sub(w_s[0][1][:, at], w_raw[0][:, at], w_s[0][0][:, at]).then_inc(early_lo, 1)
            dve.wait_ge(rows_loaded, 32)
            nc.vector.tensor_scalar(rows_sb[:, :], rows_sb[:, :], RANK, None, ALU.mult).then_inc(idx_ready, 1)
            dve.wait_ge(idx_ready, 1)
            nc.vector.tensor_tensor(idx_base[:, :], rows_sb[:, :], lane_sb[:, :].to_broadcast([P, GROUPS]), ALU.add).then_inc(idx_ready, 1)
            for j in range(1, EARLY):
                dve.wait_ge(early_hi, HC + j)
                s = j % 2
                sub(w_s[s][1][:, 0:HC * GU], w_raw[s][:, 0:HC * GU], w_s[s][0][:, 0:HC * GU]).then_inc(early_lo, 1)
            split_agu(0)
            split_gu(Step(0, 0))
            split_d(Step(0, 0))
            split_gu(Step(0, 1))
            dve.wait_ge(mask_loaded, 16)
            for m in range(MATS):
                dve.wait_ge(t_done, m + 1)
                t_split(ax_ps[m], 0, m)
            split_d(Step(0, 1))
            gated(Step(0, 0))
            split_gu(Step(0, 2))
            act_rest(Step(0, 0))
            gated(Step(0, 1))
            act_rest(Step(0, 1))
            for blk in range(BLOCKS):
                def body(st):
                    if st.blk == 0 and st.known in (0, 1):
                        return
                    if st.blk == 0 and st.known == 2:
                        gated(st)
                        split_gu(st.shift(1))
                        split_d(st)
                    else:
                        split_d(st)
                        if st.known != FC - 1:
                            split_gu(st.shift(1))
                    if st.blk and st.known in (2, 3):
                        mix(0 if st.known == 2 else 2)
                    if not (st.blk == 0 and st.known == 2):
                        gated(st)
                    act_rest(st)
                    if st.blk == 0 and st.known == 2:
                        dve.wait_ge(x_hi, 1)
                        sub(x_s[1][1][:, :, :], x_raw[:, :, :], x_s[1][0][:, :, :]).then_inc(x_lo, 1)
                        dve.wait_ge(ebias_hi_done, 1)
                        sub(ebias_lo[:, :], ebias[0:E, :], ebias_hi[0:E, :]).then_inc(ebias_lo_done, 1)
                    if st.known == 2:
                        dve.wait_ge(bd_hi, st.blk + 1)
                        sub(bd_s[1][:, :, :], bd_raw[:, :, :], bd_s[0][:, :, :]).then_inc(bd_lo, 1)
                    if st.blk and st.known == 0:
                        top_eight(PARTS[0])
                        softmax(PARTS[0])
                    if st.blk and st.known == 1:
                        rest_wt(PARTS[0])
                    if st.blk and st.known in (2, 3):
                        mix(1 if st.known == 2 else 3)
                steps(dve, blk, body)
                if blk + 1 < BLOCKS:
                    split_agu(blk + 1)
                    dve.wait_ge(td_done, GB * FC * (blk + 1))
                    t_split(td_ps, blk, 2)
                    for m in range(MATS):
                        dve.wait_ge(t_done, MATS * (blk + 1) + m + 1)
                        t_split(ax_ps[m], blk + 1, m)
                    for h in (1, 3):
                        dve.wait_ge(block_done, h + 1)
                        nc.vector.tensor_copy(down[:, h, :], down_ps[h][:, :]).then_inc(down_v, 1)
            dve.wait_ge(td_done, GB * FC * BLOCKS)
            t_split(td_ps, BLOCKS - 1, 2)
            top_eight(PARTS[1])
            softmax(PARTS[1])
            rest_wt(PARTS[1])
            top_eight(PARTS[2])
            softmax(PARTS[2])
            scale_last(PARTS[1])
            rest_wt(PARTS[2])
            mix_last(PARTS[1])
            scale_last(PARTS[2])
            mix_last(PARTS[2])

        @block.tensor
        def _(pe):
            def three(out, w, x, start=False, stop=False):
                pe.matmul(out, w[0], x[0], start=start, stop=False, skip_group_check=True)
                pe.matmul(out, w[0], x[1], start=False, stop=False, skip_group_check=True)
                return pe.matmul(out, w[1], x[0], start=False, stop=stop, skip_group_check=True)

            def both(pair, *at):
                return [t[at] for t in pair]

            ALLP = slice(None)

            def a_x_group(blk, m, g, out):
                for c in range(HC):
                    last = three(out[:, g * GT:(g + 1) * GT],
                                 both(agu_s, ALLP, m * HC + c, slice(g * P, (g + 1) * P)),
                                 both(x_s[blk], ALLP, c, slice(g * GT, (g + 1) * GT)),
                                 start=(c == 0), stop=(c == HC - 1))
                return last

            def a_x(blk, m):
                pe.wait_ge(agu_lo, GB * (blk + 1))
                pe.wait_ge(x_lo, blk)
                pe.wait_ge(t_masked, t_count(blk - 1, (0, 2)[m]))
                for g in range(GB):
                    last = a_x_group(blk, m, g, ax_ps[m])
                last.then_inc(t_done, 1)

            def w_x(blk, m, s, out, c):
                at = c * GU + m * P
                return three(out[:, :], both(w_s[s], ALLP, slice(at, at + P)), both(x_s[blk], ALLP, c, ALLP), start=(c == 0))

            def b_a_x(m, s, out):
                for g in range(GB):
                    cols = slice(g * GT, (g + 1) * GT)
                    last = three(out[:, cols], both(b_s[s], ALLP, g, slice(m * P, (m + 1) * P)), both(t_s[m], ALLP, cols),
                                 stop=(g == GB - 1))
                return last

            def project(st, m, out):
                for c in range(HC):
                    w_x(st.blk, m, st.slot, out, c)
                return b_a_x(m, st.slot, out)

            def gate(st):
                pe.wait_ge(gu_lo, st.n + 1)
                if st.known == 0:
                    pe.wait_ge(t_lo, t_count(st.blk, 1))
                pe.wait_ge(silu_done, st.n)
                project(st, 0, gate_ps).then_inc(gate_done, 1)

            def up(st):
                pe.wait_ge(mul_done, st.n)
                project(st, 1, up_ps).then_inc(up_done, 1)

            def first_steps():
                def w_parts(j, chunks):
                    st = Step(0, j)
                    for c in chunks:
                        pe.wait_ge(early_lo, c + 1 if j == 0 else HC + j)
                        for m in range(MATS):
                            last = w_x(0, m, st.slot, gu_bank(st, m), c)
                        if j == 0 and c == HC - 1:
                            last.then_inc(early_used, 1)

                def b_part(j, m):
                    st = Step(0, j)
                    pe.wait_ge(t_lo, t_count(0, m))
                    pe.wait_ge(gu_lo, j + 1)
                    b_a_x(m, st.slot, gu_bank(st, m)).then_inc((gate_done, up_done)[m], 1)

                w_parts(0, range(HC))
                w_parts(1, range(HC))
                w_parts(2, (0,))
                for k, g in enumerate(A_ORDER):
                    pe.wait_ge(agu_lo, k + 1)
                    for m in range(MATS):
                        last = a_x_group(0, m, g, ax_ps[m])
                        if k == GB - 1:
                            last.then_inc(t_done, 1)
                w_parts(2, range(1, HC - 1))
                b_part(0, 0)
                b_part(1, 0)
                b_part(0, 1)
                b_part(1, 1)
                w_parts(2, (HC - 1,))
                b_part(2, 0)
                b_part(2, 1)

            def down_step(st):
                s = st.slot
                pe.wait_ge(d_lo, st.n + 1)
                pe.wait_ge(act_lo, st.n + 1)
                first = st.known == 0
                if first and st.blk:
                    pe.wait_ge(down_v, HC // 2)
                    pe.wait_ge(down_a, HC // 2)
                for g in range(GB):
                    cols = slice(g * GT, (g + 1) * GT)
                    three(td_ps[:, cols], both(ad_s[s], ALLP, slice(g * P, (g + 1) * P)), both(act_s[s], ALLP, cols),
                          start=first and g == 0).then_inc(td_done, 1)
                very_first = first and not st.blk
                for h in (2, 3, 0, 1) if very_first else range(HC):
                    if very_first:
                        pe.wait_ge((silu_done, mul_done)[h % 2], 2 if h >= 2 else 3)
                    at = HC * GU + h * P
                    last = three(down_ps[h][:, :], both(w_s[s], ALLP, slice(at, at + P)), both(act_s[s], ALLP, ALLP), start=first)
                last.then_inc(down_done, 1)

            def b_down(part, groups):
                pe.wait_ge(bd_lo, part.blk + 1)
                pe.wait_ge(t_lo, t_count(part.blk, 2))
                for h in range(HC):
                    if part.at == 2:
                        pe.wait_ge(down_a, PARTS[1].copied(h)[1])
                    for g in groups:
                        cols = slice(g * GT, (g + 1) * GT)
                        last = three(down_ps[h][:, cols], both(bd_s, ALLP, g, slice(h * P, (h + 1) * P)), both(t_s[2], ALLP, cols),
                                     stop=True)
                    last.then_inc(block_done, 1)

            def router_logits(part):
                sums = sums_of(part)
                pe.wait_ge(small_loaded, 64)
                pe.wait_ge(ones_ready, 1)
                pe.matmul(sums[:, part.span, :], raw(ones[0:1, :]),
                          rbias[:, :].rearrange("a (o e) -> a o e", o=1).to_broadcast([1, len(part.chunks), E]),
                          start=True, stop=False, skip_group_check=True)
                for c in range(HC):
                    engine, count = part.copied(c)
                    pe.wait_ge((down_a, down_v)[engine], count)
                    for t in part.chunks:
                        last = pe.matmul(sums[:, t, :], down[:, c, t * P:(t + 1) * P], wr[:, c, :],
                                         start=False, stop=(c == HC - 1), skip_group_check=True)
                last.then_inc(logits_done, 1)

            def turn_weights(part):
                for k, t in enumerate(part.chunks):
                    pe.wait_ge(weights_done, part.turned + k + 1)
                    last = pe.transpose(aux_ps[0:E, t * P:(t + 1) * P], probs[:, t, :], ident)
                last.then_inc(wt_done, 1)

            def weight_sums(part):
                pe.wait_ge(wt_lo, part.at + 1)
                if part.at == 2:
                    pe.wait_ge(wsum_copied, part.at)
                    pe.wait_ge(scaled_v, 2)
                for out in (wsum_bank(part), gate_ps)[:2 if part.last else 1]:
                    pe.matmul(out[:, part.cols], ones[:, :], w_t[:, part.cols], start=True, stop=True).then_inc(wsum_done, 1)

            def bias_mix(part, h, out, start):
                at = slice(h * P, (h + 1) * P)
                pe.matmul(out[:, part.cols], ebias_hi[:, at], w_t[:, part.cols], start=start, stop=False, skip_group_check=True)
                pe.matmul(out[:, part.cols], ebias_lo[:, at], w_t[0:E, part.cols], start=False, stop=True,
                          skip_group_check=True).then_inc(mix_done, 1)

            def mix_earlier(h):
                if h == 0:
                    pe.wait_ge(wsum_copied, 1)
                    pe.wait_ge(ebias_lo_done, 1)
                else:
                    pe.wait_ge(mixed, h)
                bias_mix(PARTS[0], h, aux_ps, True)

            def x_onto(rows):
                for h in rows:
                    pe.wait_ge(down_a, PARTS[2].copied(h)[1])
                    for k in range(2):
                        pe.matmul(down_ps[h][:, :], ident_r[:, :], x_s[BLOCKS - 1][k][:, h, :],
                                  start=(k == 0), stop=False, skip_group_check=True)

            pe.wait_ge(ones_ready, 1)
            for _ in range(WARM_UP):
                pe.matmul(td_ps[:, :].rearrange("p (o n) -> p o n", n=P), ones[:, :],
                          ones[:, :].rearrange("p (o n) -> p o n", n=P).to_broadcast([P, BT // P, P]), start=True, stop=True)
            first_steps()
            for blk in range(BLOCKS):
                def body(st):
                    if st.early():
                        if st.known:
                            down_step(st.shift(-1))
                        return
                    gate(st)
                    if st.blk and st.known in (2, 3):
                        mix_earlier(0 if st.known == 2 else 2)
                    up(st)
                    if st.blk and st.known == 0:
                        router_logits(PARTS[0])
                    if st.blk and st.known == 1:
                        turn_weights(PARTS[0])
                    if st.blk and st.known in (2, 3):
                        mix_earlier(1 if st.known == 2 else 3)
                    if st.known != 0:
                        down_step(st.shift(-1))
                    if st.blk and st.known == 1:
                        weight_sums(PARTS[0])
                steps(pe, blk, body, tail=0)
                down_step(Step(blk, FC - 1))
                if blk + 1 < BLOCKS:
                    for m in range(MATS):
                        a_x(blk + 1, m)
                    b_down(PARTS[0], range(GB))
            first, second = PARTS[1:]
            b_down(first, (0,))
            router_logits(first)
            b_down(second, (1,))
            pe.wait_ge(ident_ready, 1)
            x_onto((0, 1))
            turn_weights(first)
            router_logits(second)
            x_onto((2, 3))
            weight_sums(first)
            for h in range(HC):
                bias_mix(first, h, down_ps[h], False)
            turn_weights(second)
            weight_sums(second)
            for h in range(HC):
                pe.wait_ge(mixed, HC * first.at + h + 1)
                bias_mix(second, h, down_ps[h], False)


def kernel(**inputs):
    import numpy as np
    import concourse.bacc as bacc
    from concourse import mybir as mb
    from concourse.bass_utils import run_bass_kernel_spmd

    pre = "L0_cond_"
    get = {k: np.ascontiguousarray(v) for k, v in inputs.items()}
    pad = FC * P

    def hidden_major(w, width):
        out = np.zeros(w.shape[:-1] + (width,), w.dtype)
        out[..., :w.shape[-1]] = w
        return out

    x_t = get["x"].reshape(TOKENS, H).T.reshape(HC, P, TOKENS).transpose(1, 0, 2)
    gu = np.stack([hidden_major(get[pre + k].T, pad).reshape(HC, P, FC, P) for k in ("W_gate", "W_up")])
    gu = gu.transpose(3, 2, 1, 0, 4).reshape(FC, P, HC * GU)
    wd = hidden_major(get[pre + "W_down"], pad).T.reshape(FC, P, H)
    w_in = np.concatenate([gu, wd], axis=2)
    a_gu = np.stack([get[pre + k][0].reshape(ADAPTERS, RANK, HC, P) for k in ("A_gate", "A_up")], axis=1)
    a_gu = a_gu.transpose(0, 4, 1, 3, 2).reshape(ADAPTERS, P, A_GU)
    a_down = hidden_major(get[pre + "A_down"][0], pad).reshape(ADAPTERS, RANK, FC, P)
    a_down = a_down.transpose(0, 3, 2, 1).reshape(ADAPTERS, P, FC * RANK)
    a_tab = np.concatenate([a_gu, a_down], axis=2)
    b_gu = np.stack([hidden_major(get[pre + k][0].transpose(0, 2, 1), pad).reshape(ADAPTERS * RANK, FC, P)
                     for k in ("B_gate", "B_up")], axis=2)
    b_tab = b_gu.transpose(1, 0, 2, 3).reshape(FC * ADAPTERS * RANK, GU)
    b_down = get[pre + "B_down"][0].transpose(0, 2, 1).reshape(ADAPTERS * RANK, H)
    adapter = get["itok_B_2_6"].reshape(1, BATCH)
    adapter_rows = np.repeat(adapter[0], RANK).reshape(GROUPS, P).T
    lane = (np.arange(P) % RANK).astype(np.int32).reshape(P, 1)
    row, col = np.arange(P)[:, None], np.arange(GT)[None, :]
    masks = np.concatenate([np.where(row // RANK == col // SEQ, LORA_SCALE, 0.0), np.eye(P)], axis=1).astype(np.float32)
    router_t = get["L0_ffn_router_weight"].T.reshape(HC, P, E).transpose(1, 0, 2)
    router_bias = get["L0_ffn_router_bias"].reshape(1, E)
    arrays = dict(x_t=x_t, adapter=adapter, adapter_rows=adapter_rows, lane=lane, masks=masks, w_in=w_in, a_tab=a_tab,
                  b_tab=b_tab, b_down_tab=b_down, router_t=router_t, router_bias=router_bias,
                  expert_bias=get["L0_ffn_expert_bias"])
    arrays = {k: np.ascontiguousarray(v) for k, v in arrays.items()}

    nc = bacc.Bacc("TRN2", target_bir_lowering=False, num_devices=1)
    args = {k: nc.dram_tensor(k, v.shape, mb.dt.from_np(v.dtype), kind="ExternalInput").ap() for k, v in arrays.items()}
    out = nc.dram_tensor("out_t", (P, HC, TOKENS), mb.dt.float32, kind="ExternalOutput").ap()
    build(nc, out_t=out, **args)
    got = run_bass_kernel_spmd(nc, [arrays], core_ids=[0]).results[0]["out_t"]
    return got.transpose(2, 1, 0).reshape(BATCH, SEQ, H)
```
